# Optimizing a Trainium2 kernel written in Bass

```python
import numpy as np
import jax
import jax.numpy as jnp

def _softmax(x, axis=-1):
    return jax.nn.softmax(x, axis=axis)

def _gelu(x):
    return jax.nn.gelu(x, approximate=True)

def _silu(x):
    return jax.nn.silu(x)

def _sigmoid(x):
    return jax.nn.sigmoid(x)

def _layernorm(x, axis=-1, eps=1e-05):
    m = jnp.mean(x, axis=axis, keepdims=True)
    v = jnp.var(x, axis=axis, keepdims=True)
    return (x - m) / jnp.sqrt(v + eps)

def _scatter_add(tgt, idx, src, axis=0):
    return tgt.at[idx].add(src)

def _segment_sum(src, seg, n):
    return jax.ops.segment_sum(src, seg, n)
kernel_name = 'mk_gnn_preln_d4_gnn_r8_7faba1'

def setup_inputs(seed: int=0):
    np.random.seed(seed)
    _w = jnp.asarray

    def _rec_inputs():
        import jax
        import jax.numpy as jnp
        _gk = jax.random.key(seed)
        x = -0.0003713 + 1 * jax.random.normal(jax.random.fold_in(_gk, 1), (6250, 128), jnp.float32)
        src = jax.random.randint(jax.random.fold_in(_gk, 2), (100000,), 0, 6250, jnp.int32)
        dst = jax.random.randint(jax.random.fold_in(_gk, 3), (100000,), 0, 6250, jnp.int32)
        _o = jnp.argsort(dst, stable=True)
        src = src[_o]
        dst = dst[_o]
        edge_attr_32 = 0.000283511 + 1.00007 * jax.random.normal(jax.random.fold_in(_gk, 11), (100000, 32), jnp.float32)
        edge_type_4 = jax.random.randint(jax.random.fold_in(_gk, 13), (100000,), 0, 4, jnp.int32)
        edge_weight = 0.000452788 + 0.999756 * jax.random.normal(jax.random.fold_in(_gk, 14), (100000,), jnp.float32)
        return (x, src, dst, edge_attr_32, edge_type_4, edge_weight)
    x, src, dst, edge_attr_32, edge_type_4, edge_weight = _rec_inputs()

    def _L0_gnn_setup():
        import jax, jax.numpy as jnp
        import numpy as np
        N = 12500
        E = 200000
        D_IN = 128
        D_OUT = 128
        EPS_GIN = 0.0
        LN_EPS = 1e-05
        PROJ_EPS = 1e-09

        def _aggregate(x, edge_index, edge_weight):
            src = edge_index[0]
            tgt = edge_index[1]
            n = x.shape[0]
            m = jax.ops.segment_max(edge_weight, tgt, num_segments=n)
            ew = jnp.exp(edge_weight - m[tgt])
            denom = jax.ops.segment_sum(ew, tgt, num_segments=n)
            w = ew / denom[tgt]
            msg = w[:, None] * x[src]
            agg = jax.ops.segment_sum(msg, tgt, num_segments=n)
            norm = jnp.linalg.norm(agg, axis=-1, keepdims=True)
            return agg / (norm + PROJ_EPS)

        def _layer_norm(h, gamma, beta):
            mu = jnp.mean(h, axis=-1, keepdims=True)
            var = jnp.var(h, axis=-1, keepdims=True)
            return gamma * (h - mu) * jax.lax.rsqrt(var + LN_EPS) + beta
        key = jax.random.key(seed)
        ks = jax.random.split(key, 9)
        x = jax.random.normal(ks[0], (N, D_IN), dtype=jnp.float32)
        edge_index = jax.random.randint(ks[1], (2, E), 0, N, dtype=jnp.int64)
        edge_weight = jax.random.normal(ks[2], (E,), dtype=jnp.float32)
        s1 = 1.0 / np.sqrt(D_IN)
        s2 = 1.0 / np.sqrt(D_OUT)
        W1 = jax.random.uniform(ks[3], (D_IN, D_OUT), jnp.float32, -s1, s1)
        b1 = jax.random.uniform(ks[4], (D_OUT,), jnp.float32, -s1, s1)
        W2 = jax.random.uniform(ks[5], (D_OUT, D_OUT), jnp.float32, -s2, s2)
        b2 = jax.random.uniform(ks[6], (D_OUT,), jnp.float32, -s2, s2)
        gamma = jnp.ones((D_OUT,), jnp.float32)
        beta = jnp.zeros((D_OUT,), jnp.float32)
        return {'x': x, 'edge_index': edge_index, 'edge_weight': edge_weight, 'W1': W1, 'b1': b1, 'W2': W2, 'b2': b2, 'gamma': gamma, 'beta': beta}
    _L0_gnn_all = _L0_gnn_setup()
    _L0_gnn_in = {k: v for k, v in _L0_gnn_all.items() if k in ('W1', 'b1', 'W2', 'b2', 'gamma', 'beta')}
    del _L0_gnn_all

    def _L1_gnn_setup():
        import jax, jax.numpy as jnp
        import numpy as np
        N_NODES = 6250
        D_FEAT = 128
        N_EDGES = 75000
        ALPHA = 0.1

        def _appnp_k1(x, edge_index):
            n = x.shape[0]
            loops = jnp.arange(n, dtype=edge_index.dtype)
            src = jnp.concatenate([edge_index[0], loops])
            dst = jnp.concatenate([edge_index[1], loops])
            ones = jnp.ones(src.shape[0], dtype=x.dtype)
            deg = jax.ops.segment_sum(ones, dst, num_segments=n)
            dinv = jnp.where(deg > 0, jax.lax.rsqrt(deg), 0.0)
            norm = dinv[src] * dinv[dst]
            agg = jax.ops.segment_sum(x[src] * norm[:, None], dst, num_segments=n)
            return (1.0 - ALPHA) * agg + ALPHA * x
        key = jax.random.key(seed)
        k1, k2 = jax.random.split(key)
        x = jax.random.normal(k1, (N_NODES, D_FEAT), dtype=jnp.float32)
        edge_index = jax.random.randint(k2, (2, N_EDGES), 0, N_NODES, dtype=jnp.int64)
        return {'x': x, 'edge_index': edge_index}
    _L1_gnn_all = _L1_gnn_setup()
    _L1_gnn_in = {k: v for k, v in _L1_gnn_all.items() if k in ()}
    del _L1_gnn_all

    def _L2_gnn_setup():
        import jax, jax.numpy as jnp
        import numpy as np
        N = 12500
        E = 80000
        D = 128
        R = 4
        ALPHA = 0.2

        def _lrelu(x):
            return jax.nn.leaky_relu(x, negative_slope=ALPHA)
        key = jax.random.key(seed)
        ks = jax.random.split(key, 14)
        s = 0.05
        return {'node_features': jax.random.normal(ks[0], (N, D), jnp.float32), 'edge_index': jax.random.randint(ks[1], (2, E), 0, N), 'edge_type': jax.random.randint(ks[2], (E,), 0, R), 'W_R': jax.random.normal(ks[3], (R, 2 * D, D), jnp.float32) * s, 'b_R': jax.random.normal(ks[4], (R, D), jnp.float32) * s, 'W_Q': jax.random.normal(ks[5], (R, D, D), jnp.float32) * s, 'b_Q': jax.random.normal(ks[6], (R, D), jnp.float32) * s, 'W_K': jax.random.normal(ks[7], (R, D, D), jnp.float32) * s, 'b_K': jax.random.normal(ks[8], (R, D), jnp.float32) * s, 'W_V': jax.random.normal(ks[9], (R, D, D), jnp.float32) * s, 'b_V': jax.random.normal(ks[10], (R, D), jnp.float32) * s, 'a_w': jax.random.normal(ks[11], (2 * D, 1), jnp.float32) * s, 'a_b': jax.random.normal(ks[12], (1,), jnp.float32) * s}
    _L2_gnn_all = _L2_gnn_setup()
    _L2_gnn_in = {k: v for k, v in _L2_gnn_all.items() if k in ('W_R', 'b_R', 'W_Q', 'b_Q', 'W_K', 'b_K', 'W_V', 'b_V', 'a_w', 'a_b')}
    del _L2_gnn_all

    def _L3_gnn_setup():
        import jax, jax.numpy as jnp
        import numpy as np
        N_NODES = 6250
        N_EDGES = 75000
        D = 128
        EDGE_D = 32
        N_LAYERS = 3
        BN_EPS = 1e-05
        key = jax.random.key(seed)
        ks = jax.random.split(key, 8)
        x = jax.random.normal(ks[0], (N_NODES, D), dtype=jnp.float32)
        edge_index = jax.random.randint(ks[1], (2, N_EDGES), 0, N_NODES, dtype=jnp.int64)
        edge_attr = jax.random.normal(ks[2], (N_EDGES, EDGE_D), dtype=jnp.float32)
        W_lin = jax.random.normal(ks[3], (N_LAYERS, EDGE_D, D), dtype=jnp.float32) * 0.05
        b_lin = jnp.zeros((N_LAYERS, D), dtype=jnp.float32)
        W1 = jax.random.normal(ks[4], (N_LAYERS, D, D), dtype=jnp.float32) * 0.05
        b1 = jnp.zeros((N_LAYERS, D), dtype=jnp.float32)
        W2 = jax.random.normal(ks[5], (N_LAYERS, D, D), dtype=jnp.float32) * 0.05
        b2 = jnp.zeros((N_LAYERS, D), dtype=jnp.float32)
        gamma = jnp.ones((N_LAYERS, D), dtype=jnp.float32)
        beta = jnp.zeros((N_LAYERS, D), dtype=jnp.float32)
        return {'x': x, 'edge_index': edge_index, 'edge_attr': edge_attr, 'W_lin': W_lin, 'b_lin': b_lin, 'W1': W1, 'b1': b1, 'W2': W2, 'b2': b2, 'gamma': gamma, 'beta': beta}
    _L3_gnn_all = _L3_gnn_setup()
    _L3_gnn_in = {k: v for k, v in _L3_gnn_all.items() if k in ('W_lin', 'b_lin', 'W1', 'b1', 'W2', 'b2', 'gamma', 'beta')}
    del _L3_gnn_all
    return {'x': x, 'src': src, 'dst': dst, 'edge_attr_32': edge_attr_32, 'edge_type_4': edge_type_4, 'edge_weight': edge_weight, 'L0_gnn_W1': _L0_gnn_in['W1'], 'L0_gnn_b1': _L0_gnn_in['b1'], 'L0_gnn_W2': _L0_gnn_in['W2'], 'L0_gnn_b2': _L0_gnn_in['b2'], 'L0_gnn_gamma': _L0_gnn_in['gamma'], 'L0_gnn_beta': _L0_gnn_in['beta'], 'L2_gnn_W_R': _L2_gnn_in['W_R'], 'L2_gnn_b_R': _L2_gnn_in['b_R'], 'L2_gnn_W_Q': _L2_gnn_in['W_Q'], 'L2_gnn_b_Q': _L2_gnn_in['b_Q'], 'L2_gnn_W_K': _L2_gnn_in['W_K'], 'L2_gnn_b_K': _L2_gnn_in['b_K'], 'L2_gnn_W_V': _L2_gnn_in['W_V'], 'L2_gnn_b_V': _L2_gnn_in['b_V'], 'L2_gnn_a_w': _L2_gnn_in['a_w'], 'L2_gnn_a_b': _L2_gnn_in['a_b'], 'L3_gnn_W_lin': _L3_gnn_in['W_lin'], 'L3_gnn_b_lin': _L3_gnn_in['b_lin'], 'L3_gnn_W1': _L3_gnn_in['W1'], 'L3_gnn_b1': _L3_gnn_in['b1'], 'L3_gnn_W2': _L3_gnn_in['W2'], 'L3_gnn_b2': _L3_gnn_in['b2'], 'L3_gnn_gamma': _L3_gnn_in['gamma'], 'L3_gnn_beta': _L3_gnn_in['beta']}

def reference(x, src, dst, edge_attr_32, edge_type_4, edge_weight, L0_gnn_W1, L0_gnn_b1, L0_gnn_W2, L0_gnn_b2, L0_gnn_gamma, L0_gnn_beta, L2_gnn_W_R, L2_gnn_b_R, L2_gnn_W_Q, L2_gnn_b_Q, L2_gnn_W_K, L2_gnn_b_K, L2_gnn_W_V, L2_gnn_b_V, L2_gnn_a_w, L2_gnn_a_b, L3_gnn_W_lin, L3_gnn_b_lin, L3_gnn_W1, L3_gnn_b1, L3_gnn_W2, L3_gnn_b2, L3_gnn_gamma, L3_gnn_beta):
    import jax
    import jax.numpy as jnp

    def _L0_gnn_ref(x, edge_index, edge_weight, W1, b1, W2, b2, gamma, beta):
        import jax, jax.numpy as jnp
        import numpy as np
        N = 12500
        E = 200000
        D_IN = 128
        D_OUT = 128
        EPS_GIN = 0.0
        LN_EPS = 1e-05
        PROJ_EPS = 1e-09

        def _aggregate(x, edge_index, edge_weight):
            src = edge_index[0]
            tgt = edge_index[1]
            n = x.shape[0]
            m = jax.ops.segment_max(edge_weight, tgt, num_segments=n)
            ew = jnp.exp(edge_weight - m[tgt])
            denom = jax.ops.segment_sum(ew, tgt, num_segments=n)
            w = ew / denom[tgt]
            msg = w[:, None] * x[src]
            agg = jax.ops.segment_sum(msg, tgt, num_segments=n)
            norm = jnp.linalg.norm(agg, axis=-1, keepdims=True)
            return agg / (norm + PROJ_EPS)

        def _layer_norm(h, gamma, beta):
            mu = jnp.mean(h, axis=-1, keepdims=True)
            var = jnp.var(h, axis=-1, keepdims=True)
            return gamma * (h - mu) * jax.lax.rsqrt(var + LN_EPS) + beta
        neigh = _aggregate(x, edge_index, edge_weight)
        combined = (1.0 + EPS_GIN) * x + neigh
        h = jnp.maximum(combined @ W1 + b1, 0.0)
        h = h @ W2 + b2
        h = _layer_norm(h, gamma, beta)
        return h

    def _L1_gnn_ref(x, edge_index):
        import jax, jax.numpy as jnp
        import numpy as np
        N_NODES = 6250
        D_FEAT = 128
        N_EDGES = 75000
        ALPHA = 0.1

        def _appnp_k1(x, edge_index):
            n = x.shape[0]
            loops = jnp.arange(n, dtype=edge_index.dtype)
            src = jnp.concatenate([edge_index[0], loops])
            dst = jnp.concatenate([edge_index[1], loops])
            ones = jnp.ones(src.shape[0], dtype=x.dtype)
            deg = jax.ops.segment_sum(ones, dst, num_segments=n)
            dinv = jnp.where(deg > 0, jax.lax.rsqrt(deg), 0.0)
            norm = dinv[src] * dinv[dst]
            agg = jax.ops.segment_sum(x[src] * norm[:, None], dst, num_segments=n)
            return (1.0 - ALPHA) * agg + ALPHA * x
        h = _appnp_k1(x, edge_index)
        return x + jax.nn.relu(h)

    def _L2_gnn_ref(node_features, edge_index, edge_type, W_R, b_R, W_Q, b_Q, W_K, b_K, W_V, b_V, a_w, a_b):
        import jax, jax.numpy as jnp
        import numpy as np
        N = 12500
        E = 80000
        D = 128
        R = 4
        ALPHA = 0.2

        def _lrelu(x):
            return jax.nn.leaky_relu(x, negative_slope=ALPHA)
        num_nodes = node_features.shape[0]
        src, tgt = (edge_index[0], edge_index[1])
        rel_in = jnp.concatenate([node_features[src], node_features[tgt]], axis=1)
        h = jnp.zeros_like(node_features)
        for r in range(R):
            mask = edge_type == r
            rel_t = _lrelu(rel_in @ W_R[r] + b_R[r])
            Q = rel_t @ W_Q[r] + b_Q[r]
            K = rel_t @ W_K[r] + b_K[r]
            V = rel_t @ W_V[r] + b_V[r]
            e = _lrelu(jnp.concatenate([Q, K], axis=1) @ a_w + a_b)[:, 0]
            e_m = jnp.where(mask, e, -1e+30)
            seg_max = jax.ops.segment_max(e_m, tgt, num_segments=num_nodes)
            seg_max = jnp.where(seg_max > -1e+29, seg_max, 0.0)
            ex = jnp.where(mask, jnp.exp(e - seg_max[tgt]), 0.0)
            denom = jax.ops.segment_sum(ex, tgt, num_segments=num_nodes)
            attn = ex / jnp.maximum(denom[tgt], 1e-16)
            h = h + jax.ops.segment_sum(V * attn[:, None], tgt, num_segments=num_nodes)
        return jax.nn.elu(h)

    def _L3_gnn_ref(x, edge_index, edge_attr, W_lin, b_lin, W1, b1, W2, b2, gamma, beta):
        import jax, jax.numpy as jnp
        import numpy as np
        N_NODES = 6250
        N_EDGES = 75000
        D = 128
        EDGE_D = 32
        N_LAYERS = 3
        BN_EPS = 1e-05
        src, dst = (edge_index[0], edge_index[1])
        n = x.shape[0]
        for l in range(W1.shape[0]):
            e = edge_attr @ W_lin[l] + b_lin[l]
            msg = jax.nn.relu(x[src] + e)
            agg = jax.ops.segment_sum(msg, dst, num_segments=n)
            h = x + agg
            h = jax.nn.relu(h @ W1[l] + b1[l]) @ W2[l] + b2[l]
            mu = jnp.mean(h, axis=0)
            var = jnp.var(h, axis=0)
            h = (h - mu) * jax.lax.rsqrt(var + BN_EPS) * gamma[l] + beta[l]
            x = jax.nn.relu(h)
        return x
    edge_index = jnp.stack([src, dst])
    h = jnp.maximum(_layernorm(x, axis=-1), 0.0)
    x = x + _L0_gnn_ref(h, edge_index, edge_weight, L0_gnn_W1, L0_gnn_b1, L0_gnn_W2, L0_gnn_b2, L0_gnn_gamma, L0_gnn_beta)
    h = jnp.maximum(_layernorm(x, axis=-1), 0.0)
    x = x + _L1_gnn_ref(h, edge_index)
    h = jnp.maximum(_layernorm(x, axis=-1), 0.0)
    x = x + _L2_gnn_ref(h, edge_index, edge_type_4, L2_gnn_W_R, L2_gnn_b_R, L2_gnn_W_Q, L2_gnn_b_Q, L2_gnn_W_K, L2_gnn_b_K, L2_gnn_W_V, L2_gnn_b_V, L2_gnn_a_w, L2_gnn_a_b)
    h = jnp.maximum(_layernorm(x, axis=-1), 0.0)
    x = x + _L3_gnn_ref(h, edge_index, edge_attr_32, L3_gnn_W_lin, L3_gnn_b_lin, L3_gnn_W1, L3_gnn_b1, L3_gnn_W2, L3_gnn_b2, L3_gnn_gamma, L3_gnn_beta)
    return x

_drawn_inputs = setup_inputs


def setup_inputs(seed=0):
    import zlib

    import numpy as np

    out = dict(_drawn_inputs(seed))
    spreads = {'L0_gnn_gamma': (1.0, 0.2),
     'L0_gnn_beta': (0.0, 0.1),
     'L3_gnn_b_lin': (0.0, 0.1),
     'L3_gnn_b1': (0.0, 0.748),
     'L3_gnn_b2': (0.0, 0.8),
     'L3_gnn_gamma': (1.0, 0.2),
     'L3_gnn_beta': (0.0, 0.1)}
    factors = {'L2_gnn_b_R': 4.202,
     'L2_gnn_W_Q': 8.0,
     'L2_gnn_b_Q': 8.0,
     'L2_gnn_W_K': 8.0,
     'L2_gnn_b_K': 8.0,
     'L2_gnn_a_w': 8.0}
    for name, (base, spread) in spreads.items():
        noise = np.random.default_rng([zlib.crc32(name.encode()), seed]).standard_normal(out[name].shape)
        drawn = base * np.exp(spread * noise) if base else spread * noise
        out[name] = jnp.asarray(drawn.astype(out[name].dtype))
    for name, factor in factors.items():
        out[name] = (out[name] * factor).astype(out[name].dtype)
    return out
```

```python
from contextlib import ExitStack

import concourse.bass as bass
from concourse import mybir

ALU = mybir.AluOpType
ACT = mybir.ActivationFunctionType
F32 = mybir.dt.float32
I32 = mybir.dt.int32
AX_X = mybir.AxisListType.X

P = 128
N = 6250
E = 100000
D = 128
TYPES = 4
ATTR = 32
LAYERS = 3
TILES = 4
BLOCK = P * TILES
NB = -(-E // BLOCK)
LAST = E - (NB - 1) * BLOCK
LAST_P = LAST // TILES
HALF = NB // 2
SLOTS = 4
ROUNDS = NB // SLOTS
NW = -(-N // P)
NPAD = NW * P
TAIL = N - (NW - 1) * P
KN = P // TYPES
KW = NPAD // KN
GW = 7
NG = NW // GW
GC = GW * P
ROW = D + D + 4
BIG = float(2.0 ** 100)
FLOOR = -float(2.0 ** 96)
LN_EPS = 1e-5
PROJ_EPS = 1e-9
LAG = 3
RING = 4

assert NB == SLOTS * ROUNDS == 2 * HALF and NW == NG * GW and LAST % TILES == 0


class Steps:

    def __init__(self, engine, sem, base=0):
        self.engine, self.sem, self.base, self.count = engine, sem, base, 0

    def mark(self, instruction):
        instruction.then_inc(self.sem, 1)
        self.count += 1
        return instruction

    def settle(self):
        self.engine.wait_ge(self.sem, self.base + self.count)

    def link(self, instruction):
        self.mark(instruction)
        self.settle()


class Gathers:

    def __init__(self, t, count):
        self.sems, self.each, self.base = t["gathered"], 16 * count, t["gathers_before"]
        t["gathers_before"] += ROUNDS * self.each

    def of(self, s, i):
        return self.sems[s], i * self.each + self.each + self.base


def wait_apart(engine, passed, *waits):
    for sem, value in waits:
        engine.wait_ge(sem, value)
    engine.sem_inc(passed, 1)


class Phase:

    def __init__(self, nc, name):
        self.nc, self.name, self.stack, self.used = nc, name, ExitStack(), []

    def __enter__(self):
        self.stack.__enter__()
        self.passed = self.sem("passed")
        return self

    def __exit__(self, *what):
        return self.stack.__exit__(*what)

    def sb(self, name, shape, dt=F32):
        return self.stack.enter_context(self.nc.sbuf_tensor(f"{self.name}_{name}", shape, dt))

    def ps(self, name, shape):
        return self.stack.enter_context(self.nc.psum_tensor(f"{self.name}_{name}", shape, F32))

    def sem(self, name):
        self.used.append(self.stack.enter_context(self.nc.semaphore(f"{self.name}_{name}")))
        return self.used[-1]

    def sems(self, name, count):
        return [self.sem(f"{name}{i}") for i in range(count)]

    def clear(self):
        for semaphore in self.used:
            self.nc.gpsimd.sem_clear(semaphore)
        self.nc.all_engine_barrier()

    def block(self):
        self.stack.callback(self.clear)
        return self.stack.enter_context(self.nc.Block())


def load_function(nc, t, function):
    nc.scalar.activation(t["spare"][:, :], t["ident"][:, 0:1], function)


def at(tensor, index):
    return tensor[:, bass.ds(index, 1), :].rearrange("p a m -> p (a m)")


def prepare(nc, w, t):
    with Phase(nc, "prep") as ph:
        di = ph.sb("dst_rows_i", [HALF, 2, BLOCK], I32)
        si = ph.sb("src_rows_i", [HALF, 2, BLOCK], I32)
        ti = ph.sb("type_rows_i", [HALF, 2, BLOCK], I32)
        wf = ph.sb("weight_rows", [HALF, 2, BLOCK])
        df = ph.sb("dst_rows", [HALF, 2, BLOCK])
        sf = ph.sb("src_rows", [HALF, 2, BLOCK])
        tf = ph.sb("type_rows", [HALF, 2, BLOCK])
        qi = ph.sb("key_window_i", [HALF, 2, BLOCK], I32)
        kf = ph.sb("key_rows", [HALF, 2, BLOCK])
        ends = ph.sb("ends", [HALF, 2, 2])
        ends_i = ph.sb("ends_i", [HALF, 2, 2], I32)
        bounds = ph.sb("bounds", [HALF, 2, 4], I32)
        bounds2 = ph.sb("bounds2", [HALF, 2, 4], I32)
        nowhere = ph.sb("nowhere", [1, BLOCK])
        lane = ph.sb("lane", [P, 1])
        wq = ph.sb("wq", [P, TYPES, D])
        wk = ph.sb("wk", [P, TYPES, D])
        bq = ph.sb("bq", [P, TYPES, D])
        bk = ph.sb("bk", [P, TYPES, D])
        aw = ph.sb("aw", [P, 2, D])
        ab = ph.sb("ab", [P, 1])
        prod = ph.sb("prod", [P, 2, TYPES, D])
        cs = ph.sb("cs", [P, 4, TYPES])
        ct = ph.sb("ct", [P, TYPES, ROW - D])
        pt = [ph.ps(f"pt{i}", [P, 2, 512]) for i in range(2)]
        pc = ph.ps("pc", [P, TYPES, D])
        loaded = ph.sem("loaded")
        weights_loaded = ph.sem("weights_loaded")
        zeroed = ph.sem("zeroed")
        consts = ph.sem("consts")
        rows_ready = ph.sem("rows_ready")
        bounds_ready = ph.sem("bounds_ready")
        stored = ph.sem("stored")
        bounds_stored = ph.sem("bounds_stored")
        transposed = ph.sem("transposed")
        copied = ph.sem("copied")
        dve_steps = ph.sem("dve_steps")
        scores_ready = ph.sem("scores_ready")
        scores_spread = ph.sem("scores_spread")
        ct_ready = ph.sem("ct_ready")
        table_stored = ph.sem("table_stored")
        x_loaded = ph.sem("x_loaded")
        block = ph.block()

        def load_rows(engine, to, array):
            engine.dma_start(to[:, 0, :], array[0:HALF * BLOCK].rearrange("(b e) -> b e", e=BLOCK)).then_inc(loaded, 16)
            engine.dma_start(to[0:HALF - 1, 1, :], array[HALF * BLOCK:(NB - 1) * BLOCK].rearrange(
                "(b e) -> b e", e=BLOCK)).then_inc(loaded, 16)
            engine.dma_start(to[HALF - 1:HALF, 1, 0:LAST], array[(NB - 1) * BLOCK:E].rearrange(
                "(b e) -> b e", b=1)).then_inc(loaded, 16)
            engine.dma_start(to[HALF - 1:HALF, 1, LAST:BLOCK], array[E - (BLOCK - LAST):E].rearrange(
                "(b e) -> b e", b=1)).then_inc(loaded, 16)

        @block.sync
        def _(sp):
            load_rows(sp, di, w["dst"])
            load_rows(sp, si, w["src"])
            load_rows(sp, ti, w["edge_type_4"])
            load_rows(sp, wf, w["edge_weight"])
            sp.wait_ge(zeroed, 1)
            sp.dma_start(t["x"][:, 0:NW - 1, :], w["x"][0:(NW - 1) * P, :].rearrange("(w p) f -> p w f", p=P)).then_inc(x_loaded, 16)
            sp.dma_start(t["x"][0:TAIL, NW - 1, :], w["x"][(NW - 1) * P:N, :]).then_inc(x_loaded, 16)
            sp.wait_ge(bounds_ready, 1)
            sp.dma_start(t["bounds_d"].rearrange("(h b) c -> b h c", h=2), bounds2[:, :, :]).then_inc(bounds_stored, 16)
            sp.wait_ge(bounds_stored, 16)
            sp.dma_start(t["bounds"][:, :], t["bounds_d"].rearrange("(o b) c -> o (b c)", o=1)).then_inc(bounds_stored, 16)
            sp.wait_ge(rows_ready, 1)
            for row, d in ((df, "dst_row"), (kf, "key_row")):
                sp.dma_start(t[d][0:HALF, :], row[:, 0, :]).then_inc(stored, 16)
                sp.dma_start(t[d][HALF:NB - 1, :], row[0:HALF - 1, 1, :]).then_inc(stored, 16)
                sp.dma_start(t[d][NB - 1:NB, 0:LAST], row[HALF - 1:HALF, 1, 0:LAST]).then_inc(stored, 16)
                sp.dma_start(t[d][NB - 1:NB, LAST:BLOCK], nowhere[:, LAST:BLOCK]).then_inc(stored, 16)
            sp.dma_start(t["weight_row"].rearrange("(h b) e -> b h e", h=2), wf[:, :, :]).then_inc(stored, 16)
            sp.wait_ge(stored, 9 * 16)
            sp.wait_ge(bounds_stored, 32)
            sp.wait_ge(x_loaded, 32)

        @block.scalar
        def _(act):
            act.dma_start(wq[:, :, :], w["L2_gnn_W_Q"].rearrange("r f o -> f r o")).then_inc(weights_loaded, 16)
            act.dma_start(wk[:, :, :], w["L2_gnn_W_K"].rearrange("r f o -> f r o")).then_inc(weights_loaded, 16)
            act.dma_start(bq[:, :, :].rearrange("p r o -> p (r o)"), w["L2_gnn_b_Q"].rearrange("(a r) o -> a (r o)", a=1).to_broadcast([P, TYPES * D])).then_inc(weights_loaded, 16)
            act.dma_start(bk[:, :, :].rearrange("p r o -> p (r o)"), w["L2_gnn_b_K"].rearrange("(a r) o -> a (r o)", a=1).to_broadcast([P, TYPES * D])).then_inc(weights_loaded, 16)
            act.dma_start(aw[:, :, :].rearrange("p h o -> p (h o)"), w["L2_gnn_a_w"].rearrange("a b -> b a").to_broadcast([P, 2 * D])).then_inc(weights_loaded, 16)
            act.dma_start(ab[:, :], w["L2_gnn_a_b"].rearrange("(a b) -> a b", a=1).to_broadcast([P, 1])).then_inc(weights_loaded, 16)
            act.wait_ge(ct_ready, 1)
            for r in range(TYPES):
                act.dma_start(t["rel_table"][r * NPAD:(r + 1) * NPAD, D:ROW].rearrange("(w p) c -> p w c", p=P),
                              ct[:, r:r + 1, :].to_broadcast([P, NW, ROW - D])).then_inc(table_stored, 16)
            act.wait_ge(table_stored, TYPES * 16)

        @block.gpsimd
        def _(pool):
            nc.gpsimd.memset(t["x"][:, NW - 1, :], 0.0).then_inc(zeroed, 1)
            nc.gpsimd.memset(t["ident"][:, :], 0.0).then_inc(consts, 1)
            pool.wait_ge(consts, 1)
            nc.gpsimd.affine_select(out=t["ident"][:, :], in_=t["ident"][:, :], compare_op=ALU.not_equal, fill=1.0,
                                    base=0, pattern=[[-1, P]], channel_multiplier=1).then_inc(consts, 1)
            nc.gpsimd.iota(t["ids"][:, :], [[P, KW]], base=0, channel_multiplier=1,
                           allow_small_or_imprecise_dtypes=True).then_inc(consts, 1)
            nc.gpsimd.iota(lane[:, :], [[0, 1]], base=0, channel_multiplier=1,
                           allow_small_or_imprecise_dtypes=True).then_inc(consts, 1)
            nc.gpsimd.memset(nowhere[:, :], -1.0).then_inc(consts, 1)

        @block.vector
        def _(dve):
            st = Steps(dve, dve_steps)
            dve.wait_ge(loaded, 16 * 16)
            st.mark(nc.vector.tensor_copy(df[:, :, :], di[:, :, :]))
            st.mark(nc.vector.tensor_copy(sf[:, :, :], si[:, :, :]))
            st.mark(nc.vector.tensor_copy(tf[:, :, :], ti[:, :, :]))
            st.link(nc.vector.tensor_scalar(qi[:, :, :], di[:, :, :], 5, None, ALU.arith_shift_right))
            st.mark(nc.vector.tensor_reduce(ends[:, :, 0:1], df[:, :, :], AX_X, ALU.min))
            st.mark(nc.vector.tensor_reduce(ends[:, :, 1:2], df[:, :, :], AX_X, ALU.max))
            st.link(nc.vector.tensor_copy(kf[:, :, :], qi[:, :, :]))
            st.mark(nc.vector.tensor_copy(ends_i[:, :, :], ends[:, :, :]))
            st.link(nc.vector.scalar_tensor_tensor(kf[:, :, :], kf[:, :, :], 96.0, df[:, :, :], ALU.mult, ALU.add))
            st.mark(nc.vector.tensor_scalar(bounds[:, :, 0:2], ends_i[:, :, :], 7, None, ALU.arith_shift_right))
            st.mark(nc.vector.tensor_scalar(bounds[:, :, 2:4], ends_i[:, :, :], 5, None, ALU.arith_shift_right))
            dve.wait_ge(consts, 5)
            nc.vector.scalar_tensor_tensor(kf[:, :, :], tf[:, :, :], float(KN), kf[:, :, :], ALU.mult, ALU.add).then_inc(rows_ready, 1)
            st.settle()
            st.mark(nc.vector.tensor_copy(bounds2[:, :, :], bounds[:, :, :]))
            st.settle()
            st.mark(nc.vector.tensor_scalar(bounds2[:, :, 1:2], bounds[:, :, 1:2], 1.0, None, ALU.add))
            nc.vector.tensor_scalar(bounds2[:, :, 3:4], bounds[:, :, 3:4], 1.0, None, ALU.add).then_inc(bounds_ready, 1)
            for q in range(TYPES):
                st.mark(nc.vector.tensor_reduce(t["same_node"][:, q * KN:(q + 1) * KN].unsqueeze(2),
                                                t["ident"][:, :].rearrange("p (k j) -> p j k", j=KN), AX_X, ALU.add))
            st.link(nc.vector.scalar_tensor_tensor(prod[0:HALF, :, :, :].rearrange("p a r o -> p a (r o)"), tf[:, :, :], float(NPAD), sf[:, :, :], ALU.mult, ALU.add))
            st.link(nc.vector.scalar_tensor_tensor(tf[:, :, :], tf[:, :, :], float(NPAD), df[:, :, :], ALU.mult, ALU.add))
            dve.wait_ge(consts, 5)
            nc.vector.tensor_scalar(lane[:, :], lane[:, :], float(LAST_P), None, ALU.is_lt).then_inc(rows_ready, 1)
            dve.wait_ge(rows_ready, 2)
            for a, to in enumerate((t["src"], t["src_rel"], t["dst_rel"], t["dst"])):
                dve.wait_ge(transposed, a + 1)
                for h in range(2):
                    last = nc.vector.tensor_copy(
                        to[:, h * HALF * TILES:(h + 1) * HALF * TILES].rearrange("p (b j) -> p j b", j=TILES),
                        pt[a % 2][:, h, 0:HALF * TILES].rearrange("p (j b) -> p j b", j=TILES))
                    st.mark(last)
                st.settle()
                nc.vector.tensor_copy(cs[:, 0, 0:1], lane[:, :]).then_inc(copied, 1)
            pads = t["dst"][:, (NB - 1) * TILES:NB * TILES]
            dve.wait_ge(copied, 4)
            st.link(nc.vector.tensor_scalar(pads, pads, 1.0, lane[:, 0:1], ALU.add, ALU.mult))
            st.link(nc.vector.tensor_scalar(pads, pads, -1.0, None, ALU.add))
            dve.wait_ge(weights_loaded, 6 * 16)
            for q, k, to in ((wq, wk, 0), (bq, bk, 2)):
                st.mark(nc.vector.tensor_tensor(prod[:, 0, :, :], q[:, :, :], aw[:, 0:1, :].to_broadcast([P, TYPES, D]), ALU.mult))
                st.link(nc.vector.tensor_tensor(prod[:, 1, :, :], k[:, :, :], aw[:, 1:2, :].to_broadcast([P, TYPES, D]), ALU.mult))
                st.link(nc.vector.tensor_reduce(cs[:, to:to + 2, :], prod[:, :, :, :], AX_X, ALU.add))
                st.link(nc.vector.tensor_tensor(cs[:, to, :], cs[:, to, :], cs[:, to + 1, :], ALU.add))
            nc.vector.tensor_scalar(cs[:, 3, :], cs[:, 2, :], ab[:, 0:1], None, ALU.add).then_inc(scores_ready, 1)
            st.mark(nc.vector.memset(ct[:, :, D:ROW - D], 0.0))
            dve.wait_ge(scores_spread, 1)
            st.mark(nc.vector.tensor_copy(ct[:, :, 0:D], pc[:, :, :]))
            st.settle()
            dve.wait_ge(scores_ready, 1)
            nc.vector.tensor_copy(ct[:, :, D:D + 1], cs[:, 3, :].unsqueeze(2)).then_inc(ct_ready, 1)

        @block.tensor
        def _(pe):
            pe.wait_ge(consts, 2)
            pe.wait_ge(rows_ready, 2)
            for a, rows in enumerate((sf, prod, tf, df)):
                if a >= 2:
                    pe.wait_ge(copied, a - 1)
                for h in range(2):
                    for j in range(TILES):
                        if a == 1:
                            tile = prod[0:HALF, h, :, :].rearrange("p r o -> p (r o)").rearrange("p (e j) -> p j e", j=TILES)[:, j, :]
                        else:
                            tile = rows[:, h, :].rearrange("p (e j) -> p j e", j=TILES)[:, j, :]
                        last = nc.tensor.transpose(pt[a % 2][:, h, j * HALF:(j + 1) * HALF], tile, t["ident"][0:HALF, 0:HALF])
                last.then_inc(transposed, 1)
            pe.wait_ge(scores_ready, 1)
            for r in range(TYPES):
                last = nc.tensor.matmul(pc[:, r, :], cs[:, 0, r:r + 1].to_broadcast([P, P]), t["ident"][:, :], start=True, stop=True)
            last.then_inc(scores_spread, 1)


def table_view(table):
    return table.rearrange("(w p) f -> p w f", p=P)


class LayerNorm:

    def __init__(self, ph, name):
        self.square = ph.sb(f"{name}_square", [P, GC])
        self.small = ph.sb(f"{name}_small", [P, 4, GW])
        self.centred = ph.sem(f"{name}_centred")
        self.squared = ph.sem(f"{name}_squared")
        self.summed = ph.sem(f"{name}_summed")
        self.rooted = ph.sem(f"{name}_rooted")

    def vector(self, nc, dve, st, i, x, h):
        s = self.small
        wide = lambda k: s[:, k, :].unsqueeze(2).to_broadcast([P, GW, D])
        st.link(nc.vector.tensor_reduce(s[:, 0, :].unsqueeze(2), x, AX_X, ALU.add))
        st.link(nc.vector.tensor_scalar(s[:, 0, :], s[:, 0, :], 1.0 / D, None, ALU.mult))
        st.settle()
        nc.vector.tensor_tensor(h, x, wide(0), ALU.subtract).then_inc(self.centred, 1)
        dve.wait_ge(self.squared, i + 1)
        st.link(nc.vector.tensor_reduce(s[:, 1, :].unsqueeze(2), self.square[:, :].rearrange("p (w f) -> p w f", f=D), AX_X, ALU.add))
        nc.vector.tensor_scalar(s[:, 2, :], s[:, 1, :], 1.0 / D, LN_EPS, ALU.mult, ALU.add).then_inc(self.summed, 1)
        dve.wait_ge(self.rooted, i + 1)
        st.link(nc.vector.reciprocal(s[:, 1, :], s[:, 3, :]))
        st.link(nc.vector.tensor_tensor(h, h, wide(1), ALU.mult))

    def scalar(self, nc, act, i, h):
        act.wait_ge(self.centred, i + 1)
        nc.scalar.activation(self.square[:, :].rearrange("p (w f) -> p w f", f=D), h, ACT.Square).then_inc(self.squared, 1)
        act.wait_ge(self.summed, i + 1)
        nc.scalar.activation(self.small[:, 3, :], self.small[:, 2, :], ACT.Sqrt).then_inc(self.rooted, 1)


def group(tensor, g):
    return tensor[:, bass.ds(g * GW, GW), :]


def first_norm(nc, w, t):
    with Phase(nc, "norm") as ph:
        ln = LayerNorm(ph, "ln")
        dve_steps = ph.sem("dve_steps")
        normed = ph.sem("normed")
        stored = ph.sem("stored")
        block = ph.block()
        per = 5

        @block.vector
        def _(dve):
            with dve.Fori(0, NG) as g:
                st = Steps(dve, dve_steps, g * per)
                ln.vector(nc, dve, st, g, group(t["x"], g), group(t["h"], g))
                assert st.count == per
                nc.vector.tensor_scalar(group(t["h"], g), group(t["h"], g), 0.0, None, ALU.max).then_inc(normed, 1)

        @block.scalar
        def _(act):
            load_function(nc, t, ACT.Sqrt)
            with act.Fori(0, NG) as g:
                ln.scalar(nc, act, g, group(t["h"], g))

        @block.sync
        def _(sp):
            with sp.Fori(0, NG) as g:
                sp.wait_ge(normed, g + 1)
                sp.dma_start(table_view(t["table"])[:, bass.ds(g * GW, GW), :], group(t["h"], g)).then_inc(stored, 16)
            sp.wait_ge(stored, NG * 16)


class Windows:

    def __init__(self, nc, t, column, windows):
        self.nc, self.bounds, self.column, self.windows = nc, t["bounds"], column, windows

    def of(self, engine, b):
        _, (lo, hi) = self.nc.values_load_multi_w_load_instructions(
            self.bounds[0:1, bass.ds(b * 4 + self.column, 2)], engines=[engine.engine], min_val=0, max_val=self.windows,
            skip_runtime_bounds_check_because="they come of the edges' targets, which are nodes")
        return lo, hi


def pool_gathers(nc, ph, block, gathered, indexed, index_ring, sources):

    @block.gpsimd
    def _(pool):
        with pool.Fori(0, ROUNDS) as i:
            for s in range(SLOTS):
                for k, (table, ring, width, slot_free, offset) in enumerate(sources):
                    wait_apart(pool, ph.passed, (indexed[s], (i + 1) * 16 * len(sources)),
                               (slot_free, i * SLOTS + s + offset))
                    for j in range(TILES):
                        nc.gpsimd.indirect_dma_start(
                            out=ring[:, s, j, 0:width], out_offset=None, in_=table,
                            in_offset=bass.IndirectOffsetOnAxis(ap=index_ring[:, s, k * TILES + j:k * TILES + j + 1], axis=0),
                        ).then_inc(gathered.sems[s], 16)


def softmax_edges(nc, w, t, rel):
    name = "rel" if rel else "soft"
    kinds = 2 if rel else 1
    windows = KW if rel else NW
    with Phase(nc, name) as ph:
        width = ROW if rel else D
        ring = ph.sb("ring", [P, SLOTS, TILES, width])
        ring2 = ph.sb("ring2", [P, SLOTS, TILES, D]) if rel else ring
        index_ring = ph.sb("index_ring", [P, SLOTS, TILES * kinds], I32)
        keys = ph.sb("keys", [P, SLOTS, BLOCK])
        scores = None if rel else ph.sb("scores", [P, SLOTS, BLOCK])
        penalty = ph.sb("penalty", [P, BLOCK])
        masked = ph.sb("masked", [P, BLOCK])
        probs = ph.sb("probs", [P, BLOCK])
        probs_t = ph.sb("probs_t", [P, BLOCK])
        junk = None if rel else ph.sb("junk", [P, BLOCK])
        prod = ph.sb("prod", [P, TILES, D]) if rel else None
        e_dot = ph.sb("e_dot", [P, TILES]) if rel else None
        e_col = ph.sb("e_col", [P, SLOTS, TILES]) if rel else None
        best = ph.sb("best", [P, 1])
        shift = ph.sb("shift", [P, 2])
        scale = ph.sb("scale", [P, 3, RING])
        running = ph.sb("running", [P, windows + 1])
        out = ph.ps("out", [P, RING, 512])
        turned = ph.ps("turned", [P, 2, BLOCK])
        spread = [ph.ps(f"spread{i}", [P, BLOCK]) for i in range(2)] if rel else None
        gathered = Gathers(t, TILES * kinds)
        indexed = ph.sems("indexed", SLOTS)
        blocks_done = ph.sem("blocks_done")
        keyed = ph.sems("keyed", SLOTS)
        keys_done = ph.sem("keys_done")
        shifted = ph.sem("shifted")
        exp_done = ph.sem("exp_done")
        counted = ph.sem("counted")
        transposed = ph.sem("transposed")
        copied = ph.sem("copied")
        multiplied = ph.sem("multiplied")
        scored = ph.sem("scored")
        penalised = ph.sem("penalised")
        spread_done = ph.sem("spread_done")
        pair_steps = ph.sem("pair_steps")
        block_steps = ph.sem("block_steps")
        init = ph.sem("init")
        block = ph.block()
        rows = 1 if rel else 2
        merge_marks = 2 if rel else 3
        pair_marks = 3 + merge_marks
        block_marks = TILES + 3

        if rel:
            sources = [(t["rel_table"], ring, ROW, scored, 1), (t["tgt_table"], ring2, D, blocks_done, 2)]
            index_of = [t["src_rel"], t["dst_rel"]]
        else:
            sources = [(t["table"], ring, D, blocks_done, 2)]
            index_of = [t["src"]]
        pool_gathers(nc, ph, block, gathered, indexed, index_ring, sources)
        limits = Windows(nc, t, 2 if rel else 0, windows)

        @block.sync
        def _(sp):
            def one_round(i):
                for s in range(SLOTS):
                    b = i * SLOTS + s
                    if i is not first_round:
                        sp.wait_ge(*gathered.of(s, i - 1))
                    for k, index in enumerate(index_of):
                        sp.dma_start(index_ring[:, s, k * TILES:(k + 1) * TILES], index[:, bass.ds(b * TILES, TILES)]).then_inc(indexed[s], 16)
                    sp.wait_ge(keys_done, b + 1)
                    row = t["key_row"] if rel else t["dst_row"]
                    sp.dma_start(keys[:, s, :], row[bass.ds(b, 1), :].to_broadcast([P, BLOCK])).then_inc(keyed[s], 16)
                    if not rel:
                        sp.dma_start(scores[:, s, :], t["weight_row"][bass.ds(b, 1), :].to_broadcast([P, BLOCK])).then_inc(keyed[s], 16)

            first_round = 0
            one_round(first_round)
            with sp.Fori(1, ROUNDS) as i:
                one_round(i)

        @block.vector
        def _(dve):
            cleared = [t["acc"][:, 0:windows + 1, :], t["den"][:, 0:windows + 1], scale[:, :, :], probs_t[:, :]]
            if not rel:
                cleared.append(t["deg"][:, :])
            for tensor in cleared:
                nc.vector.memset(tensor, 0.0).then_inc(init, 1)
            nc.vector.memset(running[:, :], -FLOOR).then_inc(init, 1)
            nc.vector.memset(turned[:, :, :], 0.0).then_inc(init, 1)
            nc.vector.memset(out[:, :, :], 0.0).then_inc(multiplied, LAG - 1)
            dve.wait_ge(init, len(cleared) + 2)
            dve.wait_ge(multiplied, LAG - 1)
            dve.sem_inc(blocks_done, SLOTS)
            dve.sem_inc(keys_done, SLOTS)
            dve.sem_inc(scored, SLOTS)
            dve.sem_inc(pair_steps, 1)
            n_reg = dve.alloc_register(f"{name}_n")
            dve.reg_mov(n_reg, 0)
            past = [dve.alloc_register(f"{name}_w{k}") for k in range(LAG)]
            for reg in past:
                dve.reg_mov(reg, windows)

            def front(n, wi, s, st, between):
                own = running[:, bass.ds(wi, 1)]
                if not rel:
                    dve.wait_ge(counted, n + 1)
                nc.vector.tensor_scalar(penalty[:, :], keys[:, s, :], t["ids"][:, bass.ds(wi, 1)], BIG, ALU.not_equal, ALU.mult).then_inc(penalised, 1)
                between()
                wait_apart(dve, ph.passed, (penalised, n + 1), (exp_done, n + 1))
                if rel:
                    score = spread[s % 2][:, :].rearrange("p (j e) -> p j e", j=TILES)
                else:
                    score = scores[:, s, :].rearrange("p (e j) -> p j e", j=TILES)
                st.link(nc.vector.tensor_tensor_reduce(
                    out=masked[:, :].rearrange("p (j e) -> p j e", j=TILES),
                    in0=score, in1=penalty[:, :].rearrange("p (e j) -> p j e", j=TILES),
                    scale=1.0, scalar=-3.0e38, op0=ALU.subtract, op1=ALU.max, accum_out=best[:, :]))
                st.link(nc.vector.scalar_tensor_tensor(shift[:, 0:1], best[:, :], -1.0, own, ALU.mult, ALU.min))
                nc.vector.tensor_tensor(shift[:, 1:2], shift[:, 0:1], own, ALU.subtract).then_inc(shifted, 1)
                st.mark(nc.vector.scalar_tensor_tensor(own, best[:, :], -1.0, own, ALU.mult, ALU.min))

            def merge(n, wi, st):
                slot = (n + RING - LAG) & (RING - 1)
                by = scale[:, 0, bass.ds(slot, 1)]
                dve.wait_ge(multiplied, n + 1)
                st.mark(nc.vector.scalar_tensor_tensor(at(t["acc"], wi), at(t["acc"], wi), by,
                                                       out[:, bass.ds(slot, 1), 0:D].rearrange("p a m -> p (a m)"), ALU.mult, ALU.add))
                st.mark(nc.vector.scalar_tensor_tensor(t["den"][:, bass.ds(wi, 1)], t["den"][:, bass.ds(wi, 1)], by,
                                                       scale[:, 1, bass.ds(slot, 1)], ALU.mult, ALU.add))
                if not rel:
                    st.mark(nc.vector.scalar_tensor_tensor(t["deg"][:, bass.ds(wi, 1)], t["deg"][:, bass.ds(wi, 1)], float(BLOCK),
                                                           scale[:, 2, bass.ds(slot, 1)], ALU.add, ALU.subtract))

            def relation(b, s, i):
                st = Steps(dve, block_steps, b * block_marks)
                dve.wait_ge(*gathered.of(s, i))
                r = ring2[:, s, :, :]
                st.link(nc.vector.tensor_tensor(r, ring[:, s, :, 0:D], r, ALU.add))
                st.mark(nc.vector.scalar_tensor_tensor(r, r, 0.2, r, ALU.mult, ALU.max))
                wait_apart(dve, ph.passed, (block_steps, st.base + st.count))
                for j in range(TILES):
                    st.mark(nc.vector.tensor_tensor_reduce(out=prod[:, j, :], in0=ring2[:, s, j, :], in1=ring[:, s, j, D:2 * D], scale=1.0,
                                                           scalar=0.0, op0=ALU.mult, op1=ALU.add, accum_out=e_dot[:, j:j + 1]))
                st.settle()
                e = e_col[:, s, :].unsqueeze(2)
                st.link(nc.vector.tensor_tensor(e, e_dot[:, :].unsqueeze(2), ring[:, s, :, 2 * D:2 * D + 1], ALU.add))
                assert st.count == block_marks
                nc.vector.scalar_tensor_tensor(e, e, 0.2, e, ALU.mult, ALU.max).then_inc(scored, 1)

            def one_block(i, s, last):
                b = i * SLOTS + s
                lo, hi = limits.of(dve, b)
                if rel and not (last and s == SLOTS - 1):
                    relation(b + 1, (s + 1) % SLOTS, i + (s + 1) // SLOTS)
                waits = [(keyed[s], i * 16 * rows + 16 * rows)]
                if rel:
                    waits.append((spread_done, b + 1))
                wait_apart(dve, ph.passed, *waits)
                with dve.Fori(lo, hi) as wi:
                    n = dve.snap(n_reg, min_val=0, max_val=NB * KW)
                    oldest = dve.snap(past[-1], min_val=0, max_val=windows)
                    st = Steps(dve, pair_steps, n * pair_marks + 1)
                    front(n, wi, s, st, lambda: merge(n, oldest, st))
                    assert st.count == pair_marks, st.count
                    for newer, older in reversed(list(zip(past, past[1:]))):
                        dve.reg_mov(older, newer)
                    dve.reg_mov(past[0], wi)
                    dve.reg_add(n_reg, n_reg, 1)
                dve.sem_inc(keys_done, 1)

            if rel:
                relation(0, 0, 0)
            with dve.Fori(0, ROUNDS - 1) as i:
                for s in range(SLOTS):
                    one_block(i, s, False)
            for s in range(SLOTS):
                one_block(ROUNDS - 1, s, True)
            for k, reg in enumerate(reversed(past)):
                n = dve.snap(n_reg, min_val=0, max_val=NB * KW)
                window = dve.snap(reg, min_val=0, max_val=windows)
                st = Steps(dve, pair_steps, n * pair_marks + 1 + k * merge_marks)
                st.settle()
                merge(n + k, window, st)

        @block.scalar
        def _(act):
            load_function(nc, t, ACT.Exp)
            act.wait_ge(multiplied, LAG - 1)
            act.sem_inc(exp_done, 1)
            act.sem_inc(counted, 1)
            n_reg = act.alloc_register(f"{name}_n_act")
            act.reg_mov(n_reg, 0)

            def copy(n):
                act.wait_ge(transposed, n + 1)
                act.wait_ge(multiplied, n + LAG - 1)
                nc.scalar.copy(probs_t[:, :], turned[:, bass.ds((n + 1) & 1, 1), :].rearrange("p a m -> p (a m)")).then_inc(copied, 1)

            def one_block(i, s, last):
                b = i * SLOTS + s
                lo, hi = limits.of(act, b)
                with act.Fori(lo, hi) as wi:
                    n = act.snap(n_reg, min_val=0, max_val=NB * KW)
                    slot = n & (RING - 1)
                    if not rel:
                        act.wait_ge(penalised, n + 1)
                        nc.scalar.activation(junk[:, :], penalty[:, :], ACT.Copy, scale=1.0 / BIG,
                                             accum_out=scale[:, 2, bass.ds(slot, 1)]).then_inc(counted, 1)
                    act.wait_ge(shifted, n + 1)
                    nc.scalar.activation(scale[:, 0, bass.ds(slot, 1)], shift[:, 1:2], ACT.Exp)
                    act.wait_ge(transposed, n + 1)
                    nc.scalar.activation(probs[:, :], masked[:, :], ACT.Exp, bias=shift[:, 0:1],
                                         accum_out=scale[:, 1, bass.ds(slot, 1)]).then_inc(exp_done, 1)
                    copy(n)
                    act.reg_add(n_reg, n_reg, 1)

            with act.Fori(0, ROUNDS - 1) as i:
                for s in range(SLOTS):
                    one_block(i, s, False)
            for s in range(SLOTS):
                one_block(ROUNDS - 1, s, True)
            copy(act.snap(n_reg, min_val=0, max_val=NB * KW))

        @block.tensor
        def _(pe):
            pe.wait_ge(multiplied, LAG - 1)
            pe.sem_inc(transposed, 1)
            n_reg = pe.alloc_register(f"{name}_n_pe")
            pe.reg_mov(n_reg, 0)
            past = pe.alloc_register(f"{name}_slot")
            pe.reg_mov(past, 0)

            def spread_scores(b, s):
                pe.wait_ge(scored, b + SLOTS + 1)
                for j in range(TILES):
                    last = nc.tensor.matmul(spread[s % 2][:, j * P:(j + 1) * P], e_col[:, s, j:j + 1].to_broadcast([P, P]),
                                            t["ident"][:, :], start=True, stop=True)
                last.then_inc(spread_done, 1)

            def multiply(n, slot):
                pe.wait_ge(copied, n + 1)
                for j in range(TILES):
                    last = nc.tensor.matmul(out[:, bass.ds((n + RING - 1) & (RING - 1), 1), 0:D].rearrange("p a m -> p (a m)"),
                                            probs_t[:, j * P:(j + 1) * P],
                                            ring2[:, bass.ds(slot, 1), j, 0:D].rearrange("p a m -> p (a m)"),
                                            start=(j == 0), stop=(j == TILES - 1))
                last.then_inc(multiplied, 1)

            def one_block(i, s, last):
                b = i * SLOTS + s
                lo, hi = limits.of(pe, b)
                if rel and not (last and s == SLOTS - 1):
                    spread_scores(b + 1, (s + 1) % SLOTS)
                wait_apart(pe, ph.passed, gathered.of(s, i))
                with pe.Fori(lo, hi) as wi:
                    n = pe.snap(n_reg, min_val=0, max_val=NB * KW)
                    slot = pe.snap(past, min_val=0, max_val=SLOTS - 1)
                    pe.wait_ge(exp_done, n + 2)
                    for j in range(TILES):
                        lt = nc.tensor.matmul(turned[:, bass.ds(n & 1, 1), j * P:(j + 1) * P].rearrange("p a m -> p (a m)"),
                                              probs[:, j * P:(j + 1) * P], t["ident"][:, :], start=True, stop=True)
                    lt.then_inc(transposed, 1)
                    multiply(n, slot)
                    pe.reg_mov(past, s)
                    pe.reg_add(n_reg, n_reg, 1)
                pe.wait_ge(multiplied, pe.snap(n_reg, min_val=0, max_val=NB * KW) + LAG - 1)
                pe.sem_inc(blocks_done, 1)

            if rel:
                spread_scores(0, 0)
            with pe.Fori(0, ROUNDS - 1) as i:
                for s in range(SLOTS):
                    one_block(i, s, False)
            for s in range(SLOTS):
                one_block(ROUNDS - 1, s, True)
            multiply(pe.snap(n_reg, min_val=0, max_val=NB * KW), SLOTS - 1)


def soft_nodes(nc, w, t):
    with Phase(nc, "softn") as ph:
        w1 = ph.sb("w1", [P, D])
        w2 = ph.sb("w2", [P, D])
        b1 = ph.sb("b1", [P, 1])
        rows = ph.sb("rows", [P, 3, D])
        a = ph.sb("a", [P, GW, D])
        sq = ph.sb("sq", [P, GW, D])
        at_ = ph.sb("at", [P, GC])
        h1 = ph.sb("h1", [P, GC])
        y = ph.sb("y", [P, GW, D])
        yc = ph.sb("yc", [P, GW, D])
        tab = ph.sb("tab", [P, 2, GW, D])
        small = ph.sb("small", [P, 6, GW])
        ptr = ph.ps("ptr", [P, 1024])
        p1 = ph.ps("p1", [P, 1024])
        p2 = ph.ps("p2", [P, 1024])
        ln1 = LayerNorm(ph, "ln1")
        ln2 = LayerNorm(ph, "ln2")
        loaded = ph.sem("loaded")
        steps = ph.sem("steps")
        scaled = ph.sem("scaled")
        squared = ph.sem("squared")
        summed = ph.sem("summed")
        rooted = ph.sem("rooted")
        combined = ph.sem("combined")
        transposed = ph.sem("transposed")
        copied = ph.sem("copied")
        first = ph.sem("first")
        activated = ph.sem("activated")
        second = ph.sem("second")
        taken = ph.sem("taken")
        degrees = ph.sem("degrees")
        degrees_rooted = ph.sem("degrees_rooted")
        tabled = ph.sem("tabled")
        stored = ph.sems("stored", 2)
        block = ph.block()
        marks = 5 + 1 + 5 + 3 + 5 + 1 + 2

        @block.sync
        def _(sp):
            sp.dma_start(w1[:, :], w["L0_gnn_W1"]).then_inc(loaded, 16)
            sp.dma_start(w2[:, :], w["L0_gnn_W2"]).then_inc(loaded, 16)
            sp.dma_start(b1[:, :], w["L0_gnn_b1"].rearrange("(p o) -> p o", o=1)).then_inc(loaded, 16)
            for k, x in enumerate(("L0_gnn_b2", "L0_gnn_gamma", "L0_gnn_beta")):
                sp.dma_start(rows[:, k, :], w[x].rearrange("(o f) -> o f", o=1).to_broadcast([P, D])).then_inc(loaded, 16)
            with sp.Fori(0, NG) as g:
                sp.wait_ge(tabled, g + 1)
                sp.dma_start(table_view(t["table"])[:, bass.ds(g * GW, GW), :],
                             tab[:, bass.ds(g & 1, 1), :, :].rearrange("p a w f -> p (a w) f")).then_inc(stored[0], 16)
                sp.wait_ge(stored[0], g * 16 + 16)
                sp.sem_inc(stored[1], 1)

        @block.vector
        def _(dve):
            dve.wait_ge(loaded, 6 * 16)
            wide = lambda k: small[:, k, :].unsqueeze(2).to_broadcast([P, GW, D])
            row = lambda k: rows[:, k:k + 1, :].to_broadcast([P, GW, D])
            with dve.Fori(0, NG) as g:
                st = Steps(dve, steps, g * marks)
                cols = bass.ds(g * GW, GW)
                st.link(nc.vector.tensor_scalar(small[:, 0, :], t["den"][:, cols], 1e-30, None, ALU.max))
                st.link(nc.vector.reciprocal(small[:, 1, :], small[:, 0, :]))
                nc.vector.tensor_tensor(a[:, :, :], group(t["acc"], g), wide(1), ALU.mult).then_inc(scaled, 1)
                dve.wait_ge(squared, g + 1)
                st.link(nc.vector.tensor_reduce(small[:, 2, :].unsqueeze(2), sq[:, :, :], AX_X, ALU.add))
                nc.vector.tensor_scalar(small[:, 3, :], small[:, 2, :], 1e-30, None, ALU.max).then_inc(summed, 1)
                dve.wait_ge(rooted, g + 1)
                st.link(nc.vector.tensor_scalar(small[:, 4, :], small[:, 4, :], PROJ_EPS, None, ALU.add))
                st.link(nc.vector.reciprocal(small[:, 5, :], small[:, 4, :]))
                st.link(nc.vector.tensor_tensor(a[:, :, :], a[:, :, :], wide(5), ALU.mult))
                nc.vector.tensor_tensor(a[:, :, :], a[:, :, :], group(t["h"], g), ALU.add).then_inc(combined, 1)
                dve.wait_ge(second, g + 1)
                nc.vector.tensor_tensor(y[:, :, :], p2[:, 0:GC].rearrange("p (w f) -> p w f", f=D), row(0), ALU.add).then_inc(taken, 1)
                dve.wait_ge(taken, g + 1)
                ln1.vector(nc, dve, st, g, y[:, :, :], yc[:, :, :])
                st.link(nc.vector.tensor_tensor(yc[:, :, :], yc[:, :, :], row(1), ALU.mult))
                st.link(nc.vector.tensor_tensor(yc[:, :, :], yc[:, :, :], row(2), ALU.add))
                st.mark(nc.vector.tensor_tensor(group(t["x"], g), group(t["x"], g), yc[:, :, :], ALU.add))
                wait_apart(dve, ph.passed, (steps, st.base + st.count))
                ln2.vector(nc, dve, st, g, group(t["x"], g), group(t["h"], g))
                st.link(nc.vector.tensor_scalar(group(t["h"], g), group(t["h"], g), 0.0, None, ALU.max))
                nc.vector.tensor_scalar(small[:, 0, :], t["deg"][:, cols], 1.0, None, ALU.add).then_inc(degrees, 1)
                dve.wait_ge(degrees_rooted, g + 1)
                st.link(nc.vector.reciprocal(small[:, 2, :], small[:, 1, :]))
                st.link(nc.vector.tensor_copy(t["dinv"][:, cols], small[:, 2, :]))
                dve.wait_ge(stored[1], g)
                nc.vector.tensor_tensor(tab[:, bass.ds(g & 1, 1), :, :].rearrange("p a w f -> p (a w) f"),
                                        group(t["h"], g), wide(2), ALU.mult).then_inc(tabled, 1)
                assert st.count == marks, st.count

        @block.scalar
        def _(act):
            act.wait_ge(loaded, 6 * 16)
            with act.Fori(0, NG) as g:
                act.wait_ge(scaled, g + 1)
                nc.scalar.activation(sq[:, :, :], a[:, :, :], ACT.Square).then_inc(squared, 1)
                act.wait_ge(summed, g + 1)
                nc.scalar.activation(small[:, 4, :], small[:, 3, :], ACT.Sqrt).then_inc(rooted, 1)
                act.wait_ge(transposed, g + 1)
                nc.scalar.copy(at_[:, :], ptr[:, 0:GC]).then_inc(copied, 1)
                act.wait_ge(first, g + 1)
                nc.scalar.activation(h1[:, :], p1[:, 0:GC], ACT.Relu, bias=b1[:, 0:1]).then_inc(activated, 1)
                ln1.scalar(nc, act, g, yc[:, :, :])
                ln2.scalar(nc, act, g, group(t["h"], g))
                act.wait_ge(degrees, g + 1)
                nc.scalar.activation(small[:, 1, :], small[:, 0, :], ACT.Sqrt).then_inc(degrees_rooted, 1)

        @block.tensor
        def _(pe):
            pe.wait_ge(loaded, 6 * 16)
            with pe.Fori(0, NG) as g:
                pe.wait_ge(combined, g + 1)
                for k in range(GW):
                    last = nc.tensor.transpose(ptr[:, k * P:(k + 1) * P], a[:, k, :], t["ident"][:, :])
                last.then_inc(transposed, 1)
                pe.wait_ge(copied, g + 1)
                nc.tensor.matmul(p1[:, 0:512], w1[:, :], at_[:, 0:512], start=True, stop=True)
                nc.tensor.matmul(p1[:, 512:GC], w1[:, :], at_[:, 512:GC], start=True, stop=True).then_inc(first, 1)
                pe.wait_ge(activated, g + 1)
                for k in range(GW):
                    last = nc.tensor.matmul(p2[:, k * P:(k + 1) * P], h1[:, k * P:(k + 1) * P], w2[:, :], start=True, stop=True)
                last.then_inc(second, 1)


def number_nodes(nc, t):
    with Phase(nc, f"number{len(t)}") as ph:
        block = ph.block()

        @block.gpsimd
        def _(pool):
            nc.gpsimd.iota(t["node_row"][:, :], [[1, NPAD]], base=0, channel_multiplier=0, allow_small_or_imprecise_dtypes=True)


def one_hot_edges(nc, w, t, layer):
    gine = layer is not None
    name = f"gine{layer}" if gine else "appnp"
    with Phase(nc, name) as ph:
        ring = ph.sb("ring", [P, SLOTS, TILES, D])
        index_ring = ph.sb("index_ring", [P, SLOTS, TILES], I32)
        onehot = ph.sb("onehot", [P, 2, TILES, P])
        out = ph.ps("out", [P, 2, 512])
        gathered = Gathers(t, TILES)
        indexed = ph.sems("indexed", SLOTS)
        blocks_done = ph.sem("blocks_done")
        multiplied = ph.sem("multiplied")
        onehot_ready = ph.sem("onehot_ready")
        merged = ph.sem("merged")
        init = ph.sem("init")
        if gine:
            attr_ring = ph.sb("attr_ring", [P, SLOTS, P])
            w_lin = ph.sb("w_lin", [P, TILES, D])
            w_zeroed = ph.sem("w_zeroed")
            from_attr = [ph.ps(f"from_attr{i}", [P, TILES, D]) for i in range(2)]
            attr_loaded = ph.sems("attr_loaded", SLOTS)
            attr_used = ph.sem("attr_used")
            w_loaded = ph.sem("w_loaded")
            joined = ph.sem("joined")
            messages = ph.sem("messages")
        else:
            attr_in = ph.sb("attr_in", [P, SLOTS, P])
            attr_turned = ph.sb("attr_turned", [P, SLOTS, P])
            turned = ph.ps("turned", [P, 2, 512])
            rows_loaded = ph.sems("rows_loaded", SLOTS)
            rows_turned = ph.sem("rows_turned")
            rows_copied = ph.sem("rows_copied")
            rows_stored = ph.sems("rows_stored", SLOTS)
        block = ph.block()
        limits = Windows(nc, t, 0, NW)
        pool_gathers(nc, ph, block, gathered, indexed, index_ring, [(t["table"], ring, D, blocks_done, 2)])

        @block.sync
        def _(sp):
            if gine:
                sp.wait_ge(w_zeroed, 1)
                for j in range(TILES):
                    sp.dma_start(w_lin[j * ATTR:(j + 1) * ATTR, j, :], w["L3_gnn_W_lin"][layer]).then_inc(w_loaded, 16)
            def one_round(i):
                for s in range(SLOTS):
                    b = i * SLOTS + s
                    if i is not first_round:
                        sp.wait_ge(*gathered.of(s, i - 1))
                    sp.dma_start(index_ring[:, s, :], t["src"][:, bass.ds(b * TILES, TILES)]).then_inc(indexed[s], 16)
                    if not gine:
                        sp.wait_ge(rows_turned, b + 1)
                        if i is last_round and s == SLOTS - 1:
                            sp.dma_start(attr_in[0:LAST_P, s, :], w["edge_attr_32"][b * BLOCK:E, :].rearrange(
                                "(p j) k -> p (j k)", j=TILES)).then_inc(rows_loaded[s], 16)
                        else:
                            sp.dma_start(attr_in[:, s, :], attr_rows[:, bass.ds(b, 1), :].rearrange("p a c -> p (a c)")).then_inc(rows_loaded[s], 16)
                    if gine:
                        sp.wait_ge(blocks_done, b + 2)
                        sp.dma_start(attr_ring[:, s, :], t["attr_t"][bass.ds(b, 1), :, :].rearrange("a k e -> k (a e)")).then_inc(attr_loaded[s], 16)

            first_round, last_round = 0, ROUNDS - 1
            attr_rows = w["edge_attr_32"][0:(NB - 1) * BLOCK, :].rearrange("(b p j) k -> p b (j k)", p=P, j=TILES)
            one_round(first_round)
            with sp.Fori(1, ROUNDS - 1) as i:
                one_round(i)
            one_round(last_round)

        @block.vector
        def _(dve):
            dve.sem_inc(blocks_done, SLOTS)
            dve.sem_inc(merged, 1)
            if gine:
                nc.vector.memset(w_lin[:, :, :], 0.0).then_inc(w_zeroed, 1)
            nc.vector.memset(t["acc"][:, 0:NW + 1, :], 0.0).then_inc(init, 1)
            nc.vector.memset(out[:, :, :], 0.0).then_inc(multiplied, 1)
            dve.wait_ge(init, 1)
            n_reg, past_reg = dve.alloc_register(f"{name}_n"), dve.alloc_register(f"{name}_past")
            dve.reg_mov(n_reg, 0)
            dve.reg_mov(past_reg, NW)

            def merge(n, wi):
                dve.wait_ge(multiplied, n + 1)
                nc.vector.tensor_tensor(at(t["acc"], wi), at(t["acc"], wi), out[:, bass.ds((n + 1) & 1, 1), 0:D].rearrange("p a m -> p (a m)"), ALU.add).then_inc(merged, 1)

            def join(b, s, i):
                dve.wait_ge(*gathered.of(s, i))
                dve.wait_ge(attr_used, b + 1)
                nc.vector.tensor_tensor(ring[:, s, :, :], from_attr[s % 2][:, :, :], ring[:, s, :, :], ALU.add).then_inc(joined, 1)

            def one_block(i, s, last):
                b = i * SLOTS + s
                lo, hi = limits.of(dve, b)
                with dve.Fori(lo, hi) as wi:
                    n = dve.snap(n_reg, min_val=0, max_val=NB * NW)
                    past = dve.snap(past_reg, min_val=0, max_val=NW)
                    dve.wait_ge(merged, n + 1)
                    nc.vector.tensor_tensor(onehot[:, bass.ds(n & 1, 1), :, :].rearrange("p a j n -> p (a j) n"),
                                            t["node_row"][:, bass.ds(wi * P, P)].unsqueeze(1).to_broadcast([P, TILES, P]),
                                            t["dst"][:, bass.ds(b * TILES, TILES)].unsqueeze(2).to_broadcast([P, TILES, P]),
                                            ALU.is_equal).then_inc(onehot_ready, 1)
                    merge(n, past)
                    dve.reg_mov(past_reg, wi)
                    dve.reg_add(n_reg, n_reg, 1)
                dve.sem_inc(blocks_done, 1)
                if gine and not (last and s == SLOTS - 1):
                    join(b + 1, (s + 1) % SLOTS, i + (s + 1) // SLOTS)

            if gine:
                join(0, 0, 0)
            with dve.Fori(0, ROUNDS - 1) as i:
                for s in range(SLOTS):
                    one_block(i, s, False)
            for s in range(SLOTS):
                one_block(ROUNDS - 1, s, True)
            n = dve.snap(n_reg, min_val=0, max_val=NB * NW)
            wait_apart(dve, ph.passed, (merged, n + 1))
            merge(n, dve.snap(past_reg, min_val=0, max_val=NW))

        @block.tensor
        def _(pe):
            n_reg = pe.alloc_register(f"{name}_n_pe")
            pe.reg_mov(n_reg, 0)

            def attributes(b, s, i):
                pe.wait_ge(attr_loaded[s], i * 16 + 16)
                if not isinstance(b, int) or b >= 2:
                    pe.wait_ge(joined, b - 1)
                nc.tensor.matmul(from_attr[s % 2][:, :, :].rearrange("p j f -> p (j f)"), attr_ring[:, s, :],
                                 w_lin[:, :, :].rearrange("p j f -> p (j f)"), start=True, stop=True).then_inc(attr_used, 1)

            def one_block(i, s, ahead):
                b = i * SLOTS + s
                lo, hi = limits.of(pe, b)
                wait_apart(pe, ph.passed, (messages, b + 1) if gine else gathered.of(s, i))
                with pe.Fori(lo, hi) as wi:
                    n = pe.snap(n_reg, min_val=0, max_val=NB * NW)
                    pe.wait_ge(onehot_ready, n + 1)
                    for j in range(TILES):
                        last = nc.tensor.matmul(out[:, bass.ds(n & 1, 1), 0:D].rearrange("p a m -> p (a m)"), ring[:, s, j, :],
                                                onehot[:, bass.ds(n & 1, 1), j, :].rearrange("p a m -> p (a m)"),
                                                start=(j == 0), stop=(j == TILES - 1))
                    last.then_inc(multiplied, 1)
                    pe.reg_add(n_reg, n_reg, 1)
                if gine and ahead:
                    attributes(b + 2, (s + 2) % SLOTS, i + (s + 2) // SLOTS)
                if not gine:
                    pe.wait_ge(rows_loaded[s], i * 16 + 16)
                    pe.wait_ge(rows_copied, b + 1)
                    nc.tensor.transpose(turned[:, s % 2, 0:P], attr_in[:, s, :], t["ident"][:, :]).then_inc(rows_turned, 1)

            if gine:
                pe.wait_ge(w_loaded, TILES * 16)
                attributes(0, 0, 0)
                attributes(1, 1, 0)
            with pe.Fori(0, ROUNDS - 1) as i:
                for s in range(SLOTS):
                    one_block(i, s, True)
            for s in range(SLOTS):
                one_block(ROUNDS - 1, s, s < SLOTS - 2)

        if not gine:
            @block.scalar
            def _(act):
                act.sem_inc(rows_turned, SLOTS)
                act.sem_inc(rows_copied, 2)
                for s in range(SLOTS):
                    act.sem_inc(rows_stored[s], 16)
                with act.Fori(0, ROUNDS) as i:
                    for s in range(SLOTS):
                        b = i * SLOTS + s
                        act.wait_ge(rows_turned, b + SLOTS + 1)
                        act.wait_ge(rows_stored[s], i * 16 + 16)
                        nc.scalar.copy(attr_turned[:, s, :], turned[:, s % 2, 0:P]).then_inc(rows_copied, 1)
                        act.wait_ge(rows_copied, b + 3)
                        act.dma_start(t["attr_t"][bass.ds(b, 1), :, :].rearrange("a k e -> k (a e)"), attr_turned[:, s, :]).then_inc(rows_stored[s], 16)
                for s in range(SLOTS):
                    act.wait_ge(rows_stored[s], ROUNDS * 16 + 16)

        if gine:
            @block.scalar
            def _(act):
                with act.Fori(0, ROUNDS) as i:
                    for s in range(SLOTS):
                        act.wait_ge(joined, i * SLOTS + s + 1)
                        nc.scalar.activation(ring[:, s, :, :], ring[:, s, :, :], ACT.Relu).then_inc(messages, 1)


def appnp_nodes(nc, w, t):
    with Phase(nc, "appn") as ph:
        wr = ph.sb("wr", [P, 2, TYPES * D])
        br = ph.sb("br", [P, TYPES * D])
        a = ph.sb("a", [P, GW, D])
        b = ph.sb("b", [P, GW, D])
        ht = ph.sb("ht", [P, GC])
        rows = ph.sb("rows", [P, 2, 2, TYPES * D])
        sums = ph.sb("sums", [P, GC])
        ptr = ph.ps("ptr", [P, 1024])
        psum_sums = ph.ps("psum_sums", [P, 1024])
        pr = [ph.ps(f"pr{i}", [P, 2, TYPES * D]) for i in range(2)]
        fetched = ph.sem("fetched")
        sums_turned = ph.sem("sums_turned")
        ln = LayerNorm(ph, "ln")
        loaded = ph.sem("loaded")
        steps = ph.sem("steps")
        mixed = ph.sem("mixed")
        relued = ph.sem("relued")
        normed = ph.sem("normed")
        transposed = ph.sem("transposed")
        copied = ph.sem("copied")
        projected = ph.sem("projected")
        source_rows = ph.sem("source_rows")
        target_rows = ph.sem("target_rows")
        stored = ph.sems("stored", 2)
        block = ph.block()
        marks = 3 + 1 + 1 + 5

        @block.sync
        def _(sp):
            for half in range(2):
                sp.dma_start(wr[:, half, :].rearrange("p (r o) -> p r o", r=TYPES),
                             w["L2_gnn_W_R"][:, half * D:(half + 1) * D, :].rearrange("r f o -> f r o")).then_inc(loaded, 16)
            sp.dma_start(br[:, :], w["L2_gnn_b_R"].rearrange("(a r) o -> a (r o)", a=1).to_broadcast([P, TYPES * D])).then_inc(loaded, 16)
            rel = t["rel_table"].rearrange("(r w p) c -> p w r c", r=TYPES, p=P)
            tgt = t["tgt_table"].rearrange("(r w p) c -> p w r c", r=TYPES, p=P)
            with sp.Fori(0, NG) as g:
                for k in range(GW):
                    wi = g * GW + k
                    par = k % 2
                    sp.wait_ge(source_rows, wi + 1)
                    sp.dma_start(rel[:, bass.ds(wi, 1), :, 0:D].rearrange("p w r c -> p (w r) c"),
                                 rows[:, par, 0, :].rearrange("p (r o) -> p r o", r=TYPES)).then_inc(stored[par], 16)
                    sp.wait_ge(target_rows, wi + 1)
                    sp.dma_start(tgt[:, bass.ds(wi, 1), :, :].rearrange("p w r c -> p (w r) c"),
                                 rows[:, par, 1, :].rearrange("p (r o) -> p r o", r=TYPES)).then_inc(stored[par], 16)
            sp.wait_ge(stored[0], NG * 4 * 32)
            sp.wait_ge(stored[1], NG * 3 * 32)

        def rows_free(engine, g, k):
            par = k % 2
            uses = 4 - 3 * par if False else (4 if par == 0 else 3)
            engine.wait_ge(stored[par], g * (uses * 32) + (k // 2) * 32)

        @block.vector
        def _(dve):
            dve.wait_ge(loaded, 48)
            with dve.Fori(0, NG) as g:
                st = Steps(dve, steps, g * marks)
                cols = bass.ds(g * GW, GW)
                dinv = t["dinv"][:, cols].unsqueeze(2).to_broadcast([P, GW, D])
                st.link(nc.vector.tensor_tensor(a[:, :, :], group(t["h"], g), dinv, ALU.mult))
                dve.wait_ge(sums_turned, g + 1)
                st.link(nc.vector.tensor_tensor(a[:, :, :], a[:, :, :], psum_sums[:, 0:GC].rearrange("p (w f) -> p w f", f=D), ALU.add))
                st.link(nc.vector.tensor_tensor(a[:, :, :], a[:, :, :], dinv, ALU.mult))
                st.link(nc.vector.tensor_scalar(b[:, :, :], group(t["h"], g), 0.1, None, ALU.mult))
                nc.vector.scalar_tensor_tensor(b[:, :, :], a[:, :, :], 0.9, b[:, :, :], ALU.mult, ALU.add).then_inc(mixed, 1)
                dve.wait_ge(relued, g + 1)
                st.link(nc.vector.tensor_tensor(b[:, :, :], b[:, :, :], group(t["h"], g), ALU.add))
                nc.vector.tensor_tensor(group(t["x"], g), group(t["x"], g), b[:, :, :], ALU.add).then_inc(mixed, 1)
                wait_apart(dve, ph.passed, (mixed, g * 2 + 2))
                ln.vector(nc, dve, st, g, group(t["x"], g), a[:, :, :])
                nc.vector.tensor_scalar(b[:, :, :], a[:, :, :], 0.0, None, ALU.max).then_inc(normed, 1)
                assert st.count == marks, st.count
                for k in range(GW):
                    dve.wait_ge(projected, g * GW + k + 1)
                    rows_free(dve, g, k)
                    nc.vector.tensor_tensor(rows[:, k % 2, 1, :], pr[k % 2][:, 1, :], br[:, :], ALU.add).then_inc(target_rows, 1)

        @block.scalar
        def _(act):
            load_function(nc, t, ACT.Sqrt)
            with act.Fori(0, NG) as g:
                nc.scalar.copy(sums[:, :], group(t["acc"], g).rearrange("p w f -> p (w f)")).then_inc(fetched, 1)
                act.wait_ge(mixed, g * 2 + 1)
                nc.scalar.activation(b[:, :, :], b[:, :, :], ACT.Relu).then_inc(relued, 1)
                ln.scalar(nc, act, g, a[:, :, :])
                act.wait_ge(transposed, g + 1)
                nc.scalar.copy(ht[:, :], ptr[:, 0:GC]).then_inc(copied, 1)
                for k in range(GW):
                    act.wait_ge(projected, g * GW + k + 1)
                    rows_free(act, g, k)
                    nc.scalar.copy(rows[:, k % 2, 0, :], pr[k % 2][:, 0, :]).then_inc(source_rows, 1)

        @block.tensor
        def _(pe):
            pe.wait_ge(loaded, 48)
            with pe.Fori(0, NG) as g:
                pe.wait_ge(fetched, g + 1)
                for k in range(GW):
                    last = nc.tensor.transpose(psum_sums[:, k * P:(k + 1) * P], sums[:, k * P:(k + 1) * P], t["ident"][:, :])
                last.then_inc(sums_turned, 1)
                pe.wait_ge(normed, g + 1)
                for k in range(GW):
                    last = nc.tensor.transpose(ptr[:, k * P:(k + 1) * P], b[:, k, :], t["ident"][:, :])
                last.then_inc(transposed, 1)
                pe.wait_ge(copied, g + 1)
                for k in range(GW):
                    wi = g * GW + k
                    if k >= 2:
                        pe.wait_ge(source_rows, wi - 1)
                        pe.wait_ge(target_rows, wi - 1)
                    nc.tensor.matmul(pr[k % 2][:, 0, :], ht[:, k * P:(k + 1) * P], wr[:, 0, :], start=True, stop=True)
                    nc.tensor.matmul(pr[k % 2][:, 1, :], ht[:, k * P:(k + 1) * P], wr[:, 1, :], start=True, stop=True).then_inc(projected, 1)
                pe.wait_ge(source_rows, g * GW + GW)
                pe.wait_ge(target_rows, g * GW + GW)


def rel_nodes(nc, w, t):
    with Phase(nc, "reln") as ph:
        wv = ph.sb("wv", [P, TYPES, D])
        bv = ph.sb("bv", [P, D])
        small = ph.sb("small", [P, 3, KW])
        a = [ph.sb(f"a{i}", [P, TYPES, P]) for i in range(2)]
        share = [ph.sb(f"share{i}", [P, P]) for i in range(2)]
        a_t = [ph.sb(f"a_t{i}", [P, TYPES, TYPES, KN]) for i in range(2)]
        ex = [ph.sb(f"ex{i}", [P, D]) for i in range(2)]
        turned = [ph.ps(f"turned{i}", [P, TYPES, TYPES, KN]) for i in range(2)]
        out = [ph.ps(f"out{i}", [P, 512]) for i in range(2)]
        loaded = ph.sem("loaded")
        steps = ph.sem("steps")
        scaled = ph.sem("scaled")
        transposed = ph.sem("transposed")
        copied = ph.sem("copied")
        summed = ph.sem("summed")
        exped = ph.sem("exped")
        block = ph.block()
        marks = 2

        def each(engine, body):
            with engine.Fori(0, NW // 2) as u:
                for par in range(2):
                    body(u * 2 + par, par, False)
            body(NW - 1, (NW - 1) % 2, True)

        @block.sync
        def _(sp):
            sp.dma_start(wv[:, :, :], w["L2_gnn_W_V"].rearrange("r f o -> f r o")).then_inc(loaded, 16)
            for r in range(TYPES):
                sp.dma_start(bv[r * KN:(r + 1) * KN, :], w["L2_gnn_b_V"][r:r + 1, :].to_broadcast([KN, D])).then_inc(loaded, 16)

        @block.vector
        def _(dve):
            st = Steps(dve, steps)
            dve.sem_inc(transposed, 1)
            dve.sem_inc(summed, 2)
            den = t["den"][:, 0:KW]
            st.link(nc.vector.tensor_scalar(small[:, 0, :], den, 1e-16, None, ALU.max))
            st.link(nc.vector.reciprocal(small[:, 1, :], small[:, 0, :]))
            st.link(nc.vector.tensor_tensor(small[:, 2, :], den, small[:, 1, :], ALU.mult))
            before = st.count

            def front(g, par):
                if g is not first_window:
                    dve.wait_ge(transposed, g)
                nc.vector.tensor_tensor(a[par][:, :, :], t["acc"][:, bass.ds(g * TYPES, TYPES), :],
                                        small[:, 1, bass.ds(g * TYPES, TYPES)].unsqueeze(2).to_broadcast([P, TYPES, D]), ALU.mult).then_inc(scaled, 1)
                if g is not first_window:
                    dve.wait_ge(summed, g + 1)
                nc.vector.tensor_tensor(share[par][:, :].rearrange("p (q n) -> p q n", n=KN), t["same_node"][:, :].rearrange("p (q n) -> p q n", n=KN),
                                        small[:, 2, bass.ds(g * TYPES, TYPES)].unsqueeze(2).to_broadcast([P, TYPES, KN]), ALU.mult).then_inc(scaled, 1)

            def body(g, par, last):
                if not last:
                    front(g + 1, 1 - par)
                st = Steps(dve, steps, g * marks + before)
                dve.wait_ge(exped, g + 1)
                st.link(nc.vector.tensor_scalar(ex[par][:, :], ex[par][:, :], 1.0, -1.0, ALU.min, ALU.add))
                st.link(nc.vector.scalar_tensor_tensor(ex[par][:, :], out[par][:, 0:D], 0.0, ex[par][:, :], ALU.max, ALU.add))
                nc.vector.tensor_tensor(at(t["x"], g), at(t["x"], g), ex[par][:, :], ALU.add)
                assert st.count == marks, st.count

            first_window = 0
            front(first_window, 0)
            each(dve, body)

        @block.scalar
        def _(act):
            load_function(nc, t, ACT.Exp)

            def copy(g, par):
                act.wait_ge(transposed, g + 2)
                act.wait_ge(summed, g + 1)
                nc.scalar.copy(a_t[par][:, :, :, :].rearrange("p r q n -> p q r n"), turned[par][:, :, :, :]).then_inc(copied, 1)

            def body(g, par, last):
                if not last:
                    copy(g + 1, 1 - par)
                act.wait_ge(summed, g + 3)
                nc.scalar.activation(ex[par][:, :], out[par][:, 0:D], ACT.Exp).then_inc(exped, 1)

            copy(0, 0)
            each(act, body)

        @block.tensor
        def _(pe):
            pe.wait_ge(loaded, 5 * 16)

            def turn(g, par):
                pe.wait_ge(scaled, g * 2 + 1)
                for q in range(TYPES):
                    last = nc.tensor.transpose(turned[par][:, q, :, :].rearrange("p r n -> p (r n)"), a[par][:, q, :], t["ident"][:, :])
                last.then_inc(transposed, 1)

            def body(g, par, last):
                if not last:
                    turn(g + 1, 1 - par)
                pe.wait_ge(copied, g + 1)
                for r in range(TYPES):
                    nc.tensor.matmul(out[par][:, 0:D], a_t[par][:, r, :, :].rearrange("p q n -> p (q n)"), wv[:, r, :], start=(r == 0), stop=False)
                pe.wait_ge(scaled, g * 2 + 2)
                nc.tensor.matmul(out[par][:, 0:D], share[par][:, :], bv[:, :], start=False, stop=True).then_inc(summed, 1)

            turn(0, 0)
            each(pe, body)


def transposed_norm(nc, w, t):
    with Phase(nc, "tnorm") as ph:
        a = ph.sb("a", [P, GW, D])
        b = ph.sb("b", [P, GW, D])
        ptr = ph.ps("ptr", [P, 1024])
        ln = LayerNorm(ph, "ln")
        steps = ph.sem("steps")
        normed = ph.sem("normed")
        transposed = ph.sem("transposed")
        copied = ph.sem("copied")
        block = ph.block()
        marks = 5

        @block.vector
        def _(dve):
            with dve.Fori(0, NG) as g:
                st = Steps(dve, steps, g * marks)
                ln.vector(nc, dve, st, g, group(t["x"], g), a[:, :, :])
                dve.wait_ge(transposed, g)
                nc.vector.tensor_scalar(b[:, :, :], a[:, :, :], 0.0, None, ALU.max).then_inc(normed, 1)
                dve.wait_ge(normed, g + 1)
                assert st.count == marks

        @block.scalar
        def _(act):
            load_function(nc, t, ACT.Sqrt)
            with act.Fori(0, NG) as g:
                ln.scalar(nc, act, g, a[:, :, :])
                act.wait_ge(transposed, g + 1)
                nc.scalar.copy(t["h"][:, bass.ds(g * GW, GW), :].rearrange("p w f -> p (w f)"), ptr[:, 0:GC]).then_inc(copied, 1)

        @block.tensor
        def _(pe):
            with pe.Fori(0, NG) as g:
                pe.wait_ge(normed, g + 1)
                pe.wait_ge(copied, g)
                for k in range(GW):
                    last = nc.tensor.transpose(ptr[:, k * P:(k + 1) * P], b[:, k, :], t["ident"][:, :])
                last.then_inc(transposed, 1)


def gine_table(nc, w, t, layer):
    final = layer == LAYERS
    with Phase(nc, f"table{layer}") as ph:
        bias = ph.sb("bias", [P, 1])
        a = [ph.sb(f"a{i}", [P, GC]) for i in range(2)]
        rows = [ph.sb(f"rows{i}", [P, GW, D]) for i in range(2)]
        ptr = [ph.ps(f"ptr{i}", [P, 1024]) for i in range(2)]
        loaded = ph.sem("loaded")
        biased = ph.sem("biased")
        transposed = ph.sem("transposed")
        copied = ph.sem("copied")
        stored = ph.sems("stored", 2)
        block = ph.block()

        @block.sync
        def _(sp):
            if not final:
                sp.dma_start(bias[:, :], w["L3_gnn_b_lin"][layer].rearrange("(p o) -> p o", o=1)).then_inc(loaded, 16)
            for g in range(NG):
                sp.wait_ge(copied, g + 1)
                if not final:
                    sp.dma_start(table_view(t["table"])[:, g * GW:(g + 1) * GW, :], rows[g % 2][:, :, :]).then_inc(stored[g % 2], 16)
                elif g < NG - 1:
                    sp.dma_start(w["out"][g * GC:(g + 1) * GC, :].rearrange("(w p) f -> p w f", p=P), rows[g % 2][:, :, :]).then_inc(stored[g % 2], 16)
                else:
                    full = (NW - 1) * P
                    sp.dma_start(w["out"][g * GC:full, :].rearrange("(w p) f -> p w f", p=P), rows[g % 2][:, 0:GW - 1, :]).then_inc(stored[g % 2], 16)
                    sp.dma_start(w["out"][full:N, :], rows[g % 2][0:TAIL, GW - 1, :]).then_inc(stored[g % 2], 16)
            sp.wait_ge(stored[0], 16 * (4 + final))
            sp.wait_ge(stored[1], 16 * 3)

        @block.scalar
        def _(act):
            if not final:
                act.wait_ge(loaded, 16)
            for g in range(NG):
                if g >= 2:
                    act.wait_ge(transposed, g - 1)
                nc.scalar.activation(a[g % 2][:, :], t["h"][:, g * GW:(g + 1) * GW, :].rearrange("p w f -> p (w f)"), ACT.Identity,
                                     **({} if final else {"bias": bias[:, 0:1]})).then_inc(biased, 1)

        @block.tensor
        def _(pe):
            for g in range(NG):
                pe.wait_ge(biased, g + 1)
                if g >= 2:
                    pe.wait_ge(copied, g - 1)
                for k in range(GW):
                    last = nc.tensor.transpose(ptr[g % 2][:, k * P:(k + 1) * P], a[g % 2][:, k * P:(k + 1) * P], t["ident"][:, :])
                last.then_inc(transposed, 1)

        @block.vector
        def _(dve):
            for g in range(NG):
                dve.wait_ge(transposed, g + 1)
                if g >= 2:
                    dve.wait_ge(stored[g % 2], 16 * (g // 2))
                got = ptr[g % 2][:, 0:GC].rearrange("p (w f) -> p w f", f=D)
                if final:
                    nc.vector.tensor_tensor(rows[g % 2][:, :, :], got, t["x"][:, g * GW:(g + 1) * GW, :], ALU.add).then_inc(copied, 1)
                else:
                    nc.vector.tensor_copy(rows[g % 2][:, :, :], got).then_inc(copied, 1)


def gine_nodes(nc, w, t, layer):
    with Phase(nc, f"ginen{layer}") as ph:
        w1 = ph.sb("w1", [P, D])
        w2 = ph.sb("w2", [P, D])
        cols = ph.sb("cols", [P, 4])
        a = ph.sb("a", [P, 2, GC])
        h1 = ph.sb("h1", [P, GC])
        z = ph.sb("z", [P, NPAD])
        sq = ph.sb("sq", [P, NPAD])
        small = ph.sb("small", [P, 8])
        p1 = ph.ps("p1", [P, 1024])
        p2 = ph.ps("p2", [P, 1024])
        loaded = ph.sem("loaded")
        steps = ph.sem("steps")
        joined = ph.sem("joined")
        first = ph.sem("first")
        activated = ph.sem("activated")
        second = ph.sem("second")
        biased = ph.sem("biased")
        centred = ph.sem("centred")
        squared = ph.sem("squared")
        summed = ph.sem("summed")
        rooted = ph.sem("rooted")
        scaled = ph.sem("scaled")
        block = ph.block()
        x_t = t["h"][:, :, :].rearrange("p w f -> p (w f)")
        acc = t["acc"][:, 0:NW, :].rearrange("p w f -> p (w f)")

        @block.sync
        def _(sp):
            sp.dma_start(w1[:, :], w["L3_gnn_W1"][layer]).then_inc(loaded, 16)
            sp.dma_start(w2[:, :], w["L3_gnn_W2"][layer]).then_inc(loaded, 16)
            for k, x in enumerate(("L3_gnn_b1", "L3_gnn_b2", "L3_gnn_gamma", "L3_gnn_beta")):
                sp.dma_start(cols[:, k:k + 1], w[x][layer].rearrange("(p o) -> p o", o=1)).then_inc(loaded, 16)

        @block.vector
        def _(dve):
            st = Steps(dve, steps)
            dve.wait_ge(loaded, 6 * 16)
            with dve.Fori(0, NG) as g:
                cut = bass.ds(g * GC, GC)
                dve.wait_ge(first, g)
                nc.vector.tensor_tensor(a[:, 0, :], x_t[:, cut], acc[:, cut], ALU.add).then_inc(joined, 1)
            dve.wait_ge(biased, NG)
            st.link(nc.vector.tensor_reduce(small[:, 0:1], z[:, 0:N], AX_X, ALU.add))
            st.link(nc.vector.tensor_scalar(small[:, 1:2], small[:, 0:1], 1.0 / N, None, ALU.mult))
            nc.vector.tensor_scalar(z[:, :], z[:, :], small[:, 1:2], None, ALU.subtract).then_inc(centred, 1)
            dve.wait_ge(squared, 1)
            nc.vector.tensor_scalar(small[:, 3:4], small[:, 2:3], 1.0 / N, LN_EPS, ALU.mult, ALU.add).then_inc(summed, 1)
            dve.wait_ge(rooted, 1)
            st.link(nc.vector.reciprocal(small[:, 5:6], small[:, 4:5]))
            nc.vector.tensor_tensor(small[:, 6:7], small[:, 5:6], cols[:, 2:3], ALU.mult).then_inc(scaled, 1)

        @block.scalar
        def _(act):
            act.wait_ge(loaded, 6 * 16)
            with act.Fori(0, NG) as g:
                act.wait_ge(first, g + 1)
                nc.scalar.activation(h1[:, :], p1[:, 0:GC], ACT.Relu, bias=cols[:, 0:1]).then_inc(activated, 1)
                act.wait_ge(second, g + 1)
                nc.scalar.activation(z[:, bass.ds(g * GC, GC)], p2[:, 0:GC], ACT.Identity, bias=cols[:, 1:2]).then_inc(biased, 1)
            act.wait_ge(centred, 1)
            nc.scalar.activation(sq[:, 0:N], z[:, 0:N], ACT.Square, accum_out=small[:, 2:3]).then_inc(squared, 1)
            act.wait_ge(summed, 1)
            nc.scalar.activation(small[:, 4:5], small[:, 3:4], ACT.Sqrt).then_inc(rooted, 1)
            act.wait_ge(scaled, 1)
            nc.scalar.activation(x_t, z[:, :], ACT.Relu, bias=cols[:, 3:4], scale=small[:, 6:7])

        @block.tensor
        def _(pe):
            pe.wait_ge(loaded, 6 * 16)
            with pe.Fori(0, NG) as g:
                pe.wait_ge(joined, g + 1)
                nc.tensor.matmul(p1[:, 0:512], w1[:, :], a[:, 0, 0:512], start=True, stop=True)
                nc.tensor.matmul(p1[:, 512:GC], w1[:, :], a[:, 0, 512:GC], start=True, stop=True).then_inc(first, 1)
                pe.wait_ge(activated, g + 1)
                pe.wait_ge(biased, g)
                nc.tensor.matmul(p2[:, 0:512], w2[:, :], h1[:, 0:512], start=True, stop=True)
                nc.tensor.matmul(p2[:, 512:GC], w2[:, :], h1[:, 512:GC], start=True, stop=True).then_inc(second, 1)


def gnn(nc, w, stop=99):
    with ExitStack() as ctx:
        def dram(name, shape, dt=F32):
            return nc.dram_tensor(name, shape, dt).ap()

        def sb(name, shape, dt=F32):
            return ctx.enter_context(nc.sbuf_tensor(name, shape, dt))

        t = {
            "table": dram("table", [NPAD, D]),
            "rel_table": dram("rel_table", [TYPES * NPAD, ROW]),
            "tgt_table": dram("tgt_table", [TYPES * NPAD, D]),
            "dst_row": dram("dst_row", [NB, BLOCK]),
            "key_row": dram("key_row", [NB, BLOCK]),
            "weight_row": dram("weight_row", [NB, BLOCK]),
            "bounds_d": dram("bounds_d", [NB, 4], I32),
            "attr_t": dram("attr_t", [NB, P, P]),
            "x": sb("x", [P, NW, D]),
            "bounds": sb("bounds", [1, NB * 4], I32),
            "src": sb("src", [P, NB * TILES], I32),
            "src_rel": sb("src_rel", [P, NB * TILES], I32),
            "dst_rel": sb("dst_rel", [P, NB * TILES], I32),
            "dst": sb("dst", [P, NB * TILES]),
            "ids": sb("ids", [P, KW]),
            "ident": sb("ident", [P, P]),
            "same_node": sb("same_node", [P, P]),
            "deg": sb("deg", [P, NW + 1]),
            "spare": sb("spare", [P, 1]),
            "dinv": sb("dinv", [P, NW]),
            "den": sb("den", [P, KW + 1]),
        }
        t["gathered"] = [ctx.enter_context(nc.semaphore(f"gathered{s}")) for s in range(SLOTS)]
        t["gathers_before"] = 0
        prepare(nc, w, t)
        with nc.sbuf_tensor("h", [P, NW, D], F32) as t["h"], nc.sbuf_tensor("acc_nodes", [P, NW + 1, D], F32) as t["acc"]:
            first_norm(nc, w, t)
            softmax_edges(nc, w, t, rel=False)
            soft_nodes(nc, w, t)
            with nc.sbuf_tensor("node_row", [P, NPAD], F32) as t["node_row"]:
                number_nodes(nc, t)
                one_hot_edges(nc, w, t, None)
            appnp_nodes(nc, w, t)
        with nc.sbuf_tensor("acc_keys", [P, KW + 1, D], F32) as t["acc"]:
            softmax_edges(nc, w, t, rel=True)
            rel_nodes(nc, w, t)
        with nc.sbuf_tensor("h_t", [P, NW, D], F32) as t["h"], nc.sbuf_tensor("acc_t", [P, NW + 1, D], F32) as t["acc"], \
                nc.sbuf_tensor("node_row_t", [P, NPAD], F32) as t["node_row"]:
            number_nodes(nc, t)
            transposed_norm(nc, w, t)
            for layer in range(LAYERS):
                gine_table(nc, w, t, layer)
                one_hot_edges(nc, w, t, layer)
                gine_nodes(nc, w, t, layer)
            gine_table(nc, w, t, LAYERS)


_INS = ["x", "src", "dst", "edge_attr_32", "edge_type_4", "edge_weight", "L0_gnn_W1", "L0_gnn_b1", "L0_gnn_W2", "L0_gnn_b2",
        "L0_gnn_gamma", "L0_gnn_beta", "L2_gnn_W_R", "L2_gnn_b_R", "L2_gnn_W_Q", "L2_gnn_b_Q", "L2_gnn_W_K", "L2_gnn_b_K",
        "L2_gnn_W_V", "L2_gnn_b_V", "L2_gnn_a_w", "L2_gnn_a_b", "L3_gnn_W_lin", "L3_gnn_b_lin", "L3_gnn_W1", "L3_gnn_b1",
        "L3_gnn_W2", "L3_gnn_b2", "L3_gnn_gamma", "L3_gnn_beta"]


def kernel(**inputs):
    import numpy as _np
    import concourse.bacc as _bacc
    from concourse import mybir as _mybir
    from concourse.bass_utils import run_bass_kernel_spmd as _run

    nc = _bacc.Bacc("TRN2", target_bir_lowering=False, num_devices=1)
    arrays, w = {}, {}
    for name in _INS:
        a = _np.ascontiguousarray(inputs[name])
        arrays[f"in_{name}"] = a
        w[name] = nc.dram_tensor(f"in_{name}", a.shape, _mybir.dt.from_np(a.dtype), kind="ExternalInput").ap()
    w["out"] = nc.dram_tensor("out_x", (N, D), F32, kind="ExternalOutput").ap()
    gnn(nc, w)
    r = _run(nc, [arrays], core_ids=[0])
    return r.results[0]["out_x"]
```
